# Optimizing a Trainium2 kernel written in Bass

```python
import numpy as np
import jax
import jax.numpy as jnp

def _softmax(x, axis=-1):
    return jax.nn.softmax(x, axis=axis)

def _gelu(x):
    return jax.nn.gelu(x, approximate=True)

def _silu(x):
    return jax.nn.silu(x)

def _sigmoid(x):
    return jax.nn.sigmoid(x)

def _layernorm(x, axis=-1, eps=1e-05):
    m = jnp.mean(x, axis=axis, keepdims=True)
    v = jnp.var(x, axis=axis, keepdims=True)
    return (x - m) / jnp.sqrt(v + eps)

def _scatter_add(tgt, idx, src, axis=0):
    return tgt.at[idx].add(src)

def _segment_sum(src, seg, n):
    return jax.ops.segment_sum(src, seg, n)
kernel_name = 'mk_adj_ffn_d1_adj_r2_c822c0'

def setup_inputs(seed: int=0):
    np.random.seed(seed)
    _w = jnp.asarray

    def _rec_inputs():
        import jax
        import jax.numpy as jnp
        _gk = jax.random.key(seed)
        x = 7.22e-05 + 1 * jax.random.normal(jax.random.fold_in(_gk, 1), (128, 128, 128), jnp.float32)
        _a = jax.random.bernoulli(jax.random.fold_in(_gk, 2), 0.0625, (128, 128, 128))
        _a = jnp.logical_or(_a, jnp.swapaxes(_a, -1, -2))
        _a = jnp.logical_or(_a, jnp.eye(128, dtype=bool))
        _af = _a.astype(jnp.float32)
        _af = _af * jax.random.uniform(jax.random.fold_in(_gk, 3), (128, 128, 128), jnp.float32, 0.05, 1)
        adj = _af
        return (x, adj)
    x, adj = _rec_inputs()

    def _L0_gnn_setup():
        import jax, jax.numpy as jnp
        import numpy as np
        B, K, H = (32, 512, 128)
        LN_EPS = 1e-05

        def layer_norm(x, gamma, beta):
            mu = jnp.mean(x, axis=-1, keepdims=True)
            var = jnp.mean(jnp.square(x - mu), axis=-1, keepdims=True)
            return (x - mu) * jax.lax.rsqrt(var + LN_EPS) * gamma + beta
        key = jax.random.key(seed)
        k1, k2, k3, k4 = jax.random.split(key, 4)
        x = jax.random.normal(k1, (B, K, H), dtype=jnp.float32)
        adj = jax.random.uniform(k2, (B, K, K), dtype=jnp.float32)
        s = 1.0 / np.sqrt(H)
        W_rel = jax.random.normal(k3, (H, H), dtype=jnp.float32) * s
        b_rel = jnp.zeros((H,), dtype=jnp.float32)
        W_root = jax.random.normal(k4, (H, H), dtype=jnp.float32) * s
        ln_gamma = jnp.ones((H,), dtype=jnp.float32)
        ln_beta = jnp.zeros((H,), dtype=jnp.float32)
        return {'x': x, 'adj': adj, 'W_rel': W_rel, 'b_rel': b_rel, 'W_root': W_root, 'ln_gamma': ln_gamma, 'ln_beta': ln_beta}
    _L0_gnn_all = _L0_gnn_setup()
    _L0_gnn_in = {k: v for k, v in _L0_gnn_all.items() if k in ('W_rel', 'b_rel', 'W_root', 'ln_gamma', 'ln_beta')}
    del _L0_gnn_all

    def _L0_ffn_setup():
        import jax, jax.numpy as jnp
        import numpy as np
        B, S, D, E, H, K = (4, 2048, 128, 8, 256, 2)
        key = jax.random.key(seed)
        ks = jax.random.split(key, 6)
        x = jax.random.normal(ks[0], (B, S, D), jnp.float32)
        Wg = jax.random.normal(ks[1], (D, E), jnp.float32) * 0.02
        bg = jnp.zeros((E,), jnp.float32)
        W1 = jax.random.normal(ks[2], (E, D, H), jnp.float32) * 0.02
        b1 = jnp.zeros((E, H), jnp.float32)
        W2 = jax.random.normal(ks[3], (E, H, D), jnp.float32) * 0.02
        b2 = jnp.zeros((E, D), jnp.float32)
        return {'x': x, 'Wg': Wg, 'bg': bg, 'W1': W1, 'b1': b1, 'W2': W2, 'b2': b2}
    _L0_ffn_all = _L0_ffn_setup()
    _L0_ffn_in = {k: v for k, v in _L0_ffn_all.items() if k in ('Wg', 'bg', 'W1', 'b1', 'W2', 'b2')}
    del _L0_ffn_all
    return {'x': x, 'adj': adj, 'L0_gnn_W_rel': _L0_gnn_in['W_rel'], 'L0_gnn_b_rel': _L0_gnn_in['b_rel'], 'L0_gnn_W_root': _L0_gnn_in['W_root'], 'L0_gnn_ln_gamma': _L0_gnn_in['ln_gamma'], 'L0_gnn_ln_beta': _L0_gnn_in['ln_beta'], 'L0_ffn_Wg': _L0_ffn_in['Wg'], 'L0_ffn_bg': _L0_ffn_in['bg'], 'L0_ffn_W1': _L0_ffn_in['W1'], 'L0_ffn_b1': _L0_ffn_in['b1'], 'L0_ffn_W2': _L0_ffn_in['W2'], 'L0_ffn_b2': _L0_ffn_in['b2']}

def reference(x, adj, L0_gnn_W_rel, L0_gnn_b_rel, L0_gnn_W_root, L0_gnn_ln_gamma, L0_gnn_ln_beta, L0_ffn_Wg, L0_ffn_bg, L0_ffn_W1, L0_ffn_b1, L0_ffn_W2, L0_ffn_b2):
    import jax
    import jax.numpy as jnp

    def _L0_gnn_ref(x, adj, W_rel, b_rel, W_root, ln_gamma, ln_beta):
        import jax, jax.numpy as jnp
        import numpy as np
        B, K, H = (32, 512, 128)
        LN_EPS = 1e-05

        def layer_norm(x, gamma, beta):
            mu = jnp.mean(x, axis=-1, keepdims=True)
            var = jnp.mean(jnp.square(x - mu), axis=-1, keepdims=True)
            return (x - mu) * jax.lax.rsqrt(var + LN_EPS) * gamma + beta
        h = layer_norm(x, ln_gamma, ln_beta)
        agg = jnp.einsum('bij,bjh->bih', adj, h)
        conv = jnp.einsum('bkh,ho->bko', agg, W_rel) + b_rel + jnp.einsum('bkh,ho->bko', h, W_root)
        return x + jax.nn.relu(conv)

    def _L0_ffn_ref(x, Wg, bg, W1, b1, W2, b2):
        import jax, jax.numpy as jnp
        import numpy as np
        B, S, D, E, H, K = (4, 2048, 128, 8, 256, 2)
        Bv, Sv, Dv = x.shape
        gate_scores = x @ Wg + bg
        _, idx = jax.lax.top_k(gate_scores, K)
        mask = jax.nn.one_hot(idx, E, dtype=x.dtype).sum(axis=-2)
        xf = x.reshape(-1, Dv)
        mf = mask.reshape(-1, E)
        h = jax.nn.gelu(jnp.einsum('td,edh->teh', xf, W1) + b1[None], approximate=False)
        y = jnp.einsum('teh,ehd->ted', h, W2) + b2[None]
        out = jnp.einsum('ted,te->td', y, mf)
        return out.reshape(Bv, Sv, Dv)
    x = x + _L0_gnn_ref(_layernorm(x, axis=-1), adj, L0_gnn_W_rel, L0_gnn_b_rel, L0_gnn_W_root, L0_gnn_ln_gamma, L0_gnn_ln_beta)
    x = x + _L0_ffn_ref(_layernorm(x, axis=-1), L0_ffn_Wg, L0_ffn_bg, L0_ffn_W1, L0_ffn_b1, L0_ffn_W2, L0_ffn_b2)
    return x

_drawn_inputs = setup_inputs


def setup_inputs(seed=0):
    import zlib

    import numpy as np

    out = dict(_drawn_inputs(seed))
    spreads = {'L0_gnn_b_rel': (0.0, 0.299),
     'L0_gnn_ln_gamma': (1.0, 0.2),
     'L0_gnn_ln_beta': (0.0, 0.1),
     'L0_ffn_bg': (0.0, 0.1),
     'L0_ffn_b1': (0.0, 0.8),
     'L0_ffn_b2': (0.0, 0.1)}
    factors = {'L0_ffn_W1': 2.962}
    for name, (base, spread) in spreads.items():
        noise = np.random.default_rng([zlib.crc32(name.encode()), seed]).standard_normal(out[name].shape)
        drawn = base * np.exp(spread * noise) if base else spread * noise
        out[name] = jnp.asarray(drawn.astype(out[name].dtype))
    for name, factor in factors.items():
        out[name] = (out[name] * factor).astype(out[name].dtype)
    return out
```

```python
from contextlib import ExitStack

import numpy as np

import concourse.bass as bass
from concourse import mybir

F32 = mybir.dt.float32
BF16 = mybir.dt.bfloat16
U32 = mybir.dt.uint32
I32 = mybir.dt.int32
ALU = mybir.AluOpType
ACT = mybir.ActivationFunctionType
AX = mybir.AxisListType

P = 128
GRAPHS = 128
TOKENS = GRAPHS * P
UB = 4
UNITS = GRAPHS // UB
DEEP = 4
QUADS = UNITS // DEEP
E = 8
HID = 256
HT = HID // P
EPS = 1e-5
PAIRS = [(a, b) for a in range(E) for b in range(a + 1, E)]
NG = len(PAIRS)
C = 256
CJ = C // P
REGION = C + TOKENS
CHUNKS = (TOKENS - NG) // C + NG
CHUNKS += -CHUNKS % DEEP
CQUADS = CHUNKS // DEEP
ROW = 132
ID, MEAN, RSTD = P, P + 1, P + 2
PACK = HID + HT * P + HT
BIG = 1e38

T_IDENT = 0
T_TRI = T_IDENT + P
T_W = T_TRI + P
T_CODE = T_W + E
T_BASE = T_CODE + NG
T_VALS = T_BASE + NG
T_CHUNK = T_VALS + 4 * NG
T_COLS = T_CHUNK + 1


def constants():
    t = np.zeros((P, T_COLS), np.float32)
    t[:, T_IDENT:T_IDENT + P] = np.eye(P)
    t[:, T_TRI:T_TRI + P] = np.triu(np.ones((P, P)), 1)
    t[:, T_W:T_W + E] = E - np.arange(E)
    t[:, T_CODE:T_CODE + NG] = [(E - a) * E + (E - b) for a, b in PAIRS]
    t[:, T_BASE:T_BASE + NG] = [g * REGION + C for g in range(NG)]
    t[:, T_VALS + NG:T_VALS + 2 * NG] = [a for a, b in PAIRS]
    t[:, T_VALS + 2 * NG:T_VALS + 3 * NG] = [b for a, b in PAIRS]
    t[:, T_VALS + 3 * NG:T_VALS + 4 * NG] = np.arange(NG)
    t[:, T_CHUNK] = np.arange(P)
    ids = (np.arange(P)[:, None] + P * np.arange(GRAPHS)[None, :]).astype(np.uint32)
    pad = np.zeros((P, CJ * ROW), np.uint32)
    pad[:, ID::ROW] = TOKENS
    return t, ids, pad


def back(k, q, d):
    return (k, q - d) if q >= d else (k - 1, q - d + DEEP)


def exists(k, q, d, n):
    return not isinstance(k, int) or 0 <= DEEP * k + q - d < n


def build(nc, x, adj, W_rel, b_rel, W_root, gamma, beta, Wg, bg, W1, b1, W2, b2, table, ids, pad, out):
    rows_dram = nc.dram_tensor("rows_by_group", [NG * REGION, ROW], F32, kind="Internal").ap()

    with ExitStack() as ctx:
        def sb(name, shape, dt=F32):
            return ctx.enter_context(nc.sbuf_tensor(name, shape, dt))

        def sem(name):
            return ctx.enter_context(nc.semaphore(name))

        def sems(name, n):
            return [sem(f"{name}{i}") for i in range(n)]

        tab = sb("tab", [P, T_COLS])
        ident = tab[:, T_IDENT:T_IDENT + P]
        tok_ids = sb("tok_ids", [P, GRAPHS], U32)
        pad_rows = sb("pad_rows", [P, CJ * ROW], U32)
        tri = sb("tri", [P, P], BF16)
        tri_rest = sb("tri_rest", [P, P], BF16)
        ones = sb("ones", [P, P], BF16)
        ones_row = sb("ones_row", [1, P])
        base_row = sb("base_row", [1, UB, NG])
        w_rel = sb("w_rel", [P, P])
        w_root = sb("w_root", [P, P])
        brel_row = sb("brel_row", [1, UB * P])
        gam = sb("gam", [P, 1])
        bet = sb("bet", [P, 1])
        wg = sb("wg", [P, E])
        bgb = sb("bgb", [P, E])
        experts = sb("experts", [P, E, PACK])
        b2b = sb("b2b", [P, E, P])
        b2_pair = sb("b2_pair", [P, NG, P])

        xin = sb("xin", [P, DEEP, UB, P])
        ain = sb("ain", [P, DEEP, UB, P])
        st1 = sb("st1", [P, 2, UB, 6])
        mv1 = sb("mv1", [P, 2, UB, 2])
        var1 = sb("var1", [P, 2, 2, UB])
        std1 = sb("std1", [P, 2, 2, UB])
        rs1 = sb("rs1", [P, 2, 2, UB])
        xr_scale = sb("xr_scale", [P, 2, UB])
        xr_bias = sb("xr_bias", [P, 2, UB])
        z = sb("z", [P, 2, UB, P])
        hT = sb("hT", [P, 2, UB, P])
        aT = sb("aT", [P, 2, UB, P])
        pr = sb("pr", [P, 2, UB, P])
        xr = sb("xr", [P, 2, UB, P])
        row = sb("row", [P, DEEP, UB, ROW])
        row_u = row[:, :, :, :].bitcast(U32)
        st2 = sb("st2", [P, 2, UB, 6])
        mv2 = sb("mv2", [P, 2, UB, 2])
        var2 = sb("var2", [P, 2, UB])
        std2 = sb("std2", [P, 2, UB])
        xn = sb("xn", [P, 2, UB, P])
        xnT = sb("xnT", [P, 2, UB, P])
        g1 = sb("g1", [P, UB, E])
        g2 = sb("g2", [P, UB, E])
        eq = sb("eq", [P, UB, E])
        eqw = sb("eqw", [P, UB, E])
        m1 = sb("m1", [P, UB])
        m2 = sb("m2", [P, UB])
        w1 = sb("w1", [P, UB])
        w2 = sb("w2", [P, UB])
        wx = sb("wx", [P, UB])
        wn = sb("wn", [P, UB])
        code = sb("code", [P, UB])
        onehot = sb("onehot", [P, 2, UB, NG], BF16)
        rank_m = sb("rank_m", [P, UB, NG])
        pos = sb("pos", [P, DEEP, UB], U32)

        cnt = sb("cnt", [P, NG])
        cnt_up = sb("cnt_up", [P, NG], I32)
        nch_i = sb("nch_i", [P, NG], I32)
        nch = sb("nch", [P, NG])
        zero_g = sb("zero_g", [P, NG])
        c_end = sb("c_end", [P, NG])
        c_beg = sb("c_beg", [P, NG])
        in_beg = sb("in_beg", [P, NG])
        in_end = sb("in_end", [P, NG])
        in_g = sb("in_g", [P, NG])
        at = sb("at", [P, NG])
        last_at = sb("last_at", [P, NG])
        near = sb("near", [P, NG])
        picked = sb("picked", [P, 4, NG])
        chunk_cols = sb("chunk_cols", [P, 4], I32)
        chunk_tab = sb("chunk_tab", [1, CHUNKS * 4], I32)

        rows = sb("rows", [P, DEEP, CJ, ROW])
        rows_u = rows[:, :, :, :].bitcast(U32)
        wbuf = sb("wbuf", [P, DEEP, 2, PACK])
        xs = sb("xs", [P, 2, CJ, P])
        xsT = sb("xsT", [P, 2, C])
        xb = sb("xb", [P, DEEP, CJ, P])
        gT = sb("gT", [P, 2, 2, HT, C])
        ob = sb("ob", [P, DEEP, CJ, P])

        bank = [ctx.enter_context(nc.psum_tensor(f"bank{i}", [P, 512], F32)) for i in range(8)]

        def four(b):
            return b[:, :].rearrange("p (b c) -> p b c", b=UB)

        ps_z, ps_a, ps_p, ps_x = four(bank[0]), four(bank[1]), four(bank[2]), four(bank[5])
        ps_c = [four(bank[3]), four(bank[4])]
        ps_g = bank[6][:, 0:UB * E].rearrange("p (b e) -> p b e", b=UB)
        ps_r = bank[7][:, 0:UB * NG].rearrange("p (b g) -> p b g", b=UB)
        ps_xs = [bank[0][:, 0:C], bank[7][:, 0:C]]
        ps_h = [[bank[1 + 2 * t + s][:, :].rearrange("p (k c) -> p k c", k=HT) for s in range(2)] for t in range(2)]
        ps_y = [bank[5 + t][:, 0:C].rearrange("p (j c) -> p j c", j=CJ) for t in range(2)]

        s_tab = sem("tables_in")
        s_small = sem("small_weights_in")
        s_exp = sem("experts_in")
        s_pad = sem("padding_rows_out")
        s_ready = sem("constants_built")
        s_setup = sem("setup_step")
        s_b2 = sem("b2_pairs_built")
        s_x = sems("x_in", DEEP)
        s_adj = sems("adj_in", DEEP)
        s_ln1 = sem("ln1_step")
        s_var1 = sem("var1_ready")
        s_std1 = sem("std1_ready")
        s_coef = sem("residual_coefs_ready")
        s_z = sem("z_ready")
        s_psz = sem("zT_in_psum")
        s_psa = sem("adjT_in_psum")
        s_hT = sem("hT_ready")
        s_aT = sem("adjT_ready")
        s_psp = sem("h_wrel_in_psum")
        s_pr = sem("h_wrel_ready")
        s_conv = sem("conv_in_psum")
        s_xr = sem("residual_ready")
        s_x1 = sem("x1_ready")
        s_ln2 = sem("ln2_step")
        s_var2 = sem("var2_ready")
        s_std2 = sem("std2_ready")
        s_rstd = sem("rstd2_ready")
        s_xn = sem("xn_ready")
        s_psx = sem("xnT_in_psum")
        s_xnT = sem("xnT_ready")
        s_gate = sem("gates_in_psum")
        s_gread = sem("gates_read")
        s_top = sem("top2_step")
        s_hot = sem("onehot_ready")
        s_rank = sem("ranks_in_psum")
        s_rread = sem("ranks_read")
        s_cnt = sem("counts_in_psum")
        s_pos = sem("positions_ready")
        s_rid = sem("row_ids_ready")
        s_scat = sems("rows_scattered", DEEP)
        s_tb = sem("chunk_table_step")
        s_tbd = sem("chunk_table_ready")
        s_tbm = sem("chunk_table_in_row")
        s_rows = sems("rows_in", DEEP)
        s_w = sem("weights_copied")
        s_xs = sem("chunk_normed")
        s_xb = sem("chunk_residual_ready")
        s_psxs = sem("chunk_xT_in_psum")
        s_xsT = sem("chunk_xT_ready")
        s_h = sem("hidden_in_psum")
        s_gel = sem("gelu_ready")
        s_y = sem("y_in_psum")
        s_ob = sem("out_rows_ready")
        s_out = sems("out_rows_scattered", DEEP)

        s_turn_pool = sem("pool_wait_done")
        s_turn_dve = sem("dve_wait_done")

        SMALL = 8
        block = ctx.enter_context(nc.Block())

        @block.sync
        def _(sp):
            sp.dma_start(tab[:, :], table).then_inc(s_tab, 16)

            def load(k, q, back_exists):
                if back_exists:
                    sp.wait_ge(s_xr, DEEP * (k - 1) + q + 1)
                    sp.wait_ge(s_z, DEEP * (k - 1) + q + 1)
                sp.dma_start(xin[:, q], x[bass.ds(UB * DEEP * k + UB * q, UB)].rearrange("b p c -> p b c"))\
                    .then_inc(s_x[q], 16)
                if back_exists:
                    sp.wait_ge(s_psa, DEEP * (k - 1) + q + 1)
                sp.dma_start(ain[:, q], adj[bass.ds(UB * DEEP * k + UB * q, UB)].rearrange("b p c -> p b c"))\
                    .then_inc(s_adj[q], 16)

            for q in range(DEEP):
                load(0, q, False)
            with sp.Fori(1, QUADS) as k:
                for q in range(DEEP):
                    load(k, q, True)

            sp.wait_ge(s_tbd, 1)
            sp.dma_start(chunk_tab[0:1, :].rearrange("o (c v) -> o c v", v=4), chunk_cols[0:CHUNKS, :])\
                .then_inc(s_tbm, 16)
            sp.wait_ge(s_tbm, 16)
            sp.wait_ge(s_pad, 16)
            for q in range(DEEP):
                sp.wait_ge(s_scat[q], 16 * UB * QUADS)

            def load_rows(k, q, back_exists):
                if back_exists:
                    sp.wait_ge(s_out[q], 16 * CJ * k)
                first = sp.value_load(chunk_tab[0:1, bass.ds(4 * (DEEP * k + q), 1)], min_val=0,
                                      max_val=NG * REGION - C)
                sp.dma_start(rows[:, q], rows_dram[bass.ds(first, C)].rearrange("(p j) c -> p j c", j=CJ))\
                    .then_inc(s_rows[q], 16)

            for q in range(DEEP):
                load_rows(0, q, False)
            with sp.Fori(1, CQUADS) as k:
                for q in range(DEEP):
                    load_rows(k, q, True)
            for q in range(DEEP):
                sp.wait_ge(s_out[q], 16 * CJ * CQUADS)

        @block.gpsimd
        def _(pool):
            pool.memset(ones[:, :], 1.0).then_inc(s_ready, 1)
            pool.memset(ones_row[:, :], 1.0).then_inc(s_ready, 1)
            pool.memset(zero_g[:, :], 0.0).then_inc(s_ready, 1)
            pool.memset(row[:, :, :, RSTD + 1:ROW], 0.0).then_inc(s_ready, 1)
            pool.wait_ge(s_small, 16 * SMALL)

            def scatter(k, q, back_exists):
                if back_exists:
                    pool.wait_ge(s_scat[q], 16 * UB * k)
                pool.sem_inc(s_turn_pool, 1)
                pool.tensor_copy(row_u[:, q, :, ID], tok_ids[:, bass.ds(UB * DEEP * k + UB * q, UB)])\
                    .then_inc(s_rid, 1)
                pool.wait_ge(s_rid, DEEP * k + q + 1)
                pool.wait_ge(s_rstd, DEEP * k + q + 1)
                pool.wait_ge(s_pos, DEEP * k + q + 1)
                pool.sem_inc(s_turn_pool, 1)
                for b in range(UB):
                    pool.indirect_dma_start(rows_dram, bass.IndirectOffsetOnAxis(ap=pos[:, q, b:b + 1], axis=0),
                                            row[:, q, b], None).then_inc(s_scat[q], 16)

            for q in range(DEEP):
                scatter(0, q, False)
            with pool.Fori(1, QUADS) as k:
                for q in range(DEEP):
                    scatter(k, q, True)

            def scatter_out(k, q):
                pool.wait_ge(s_ob, DEEP * k + q + 1)
                pool.sem_inc(s_turn_pool, 1)
                for j in range(CJ):
                    pool.indirect_dma_start(out, bass.IndirectOffsetOnAxis(ap=rows_u[:, q, j, ID:ID + 1], axis=0),
                                            ob[:, q, j], None, bounds_check=TOKENS - 1, oob_is_err=False)\
                        .then_inc(s_out[q], 16)

            with pool.Fori(0, CQUADS) as k:
                for q in range(DEEP):
                    scatter_out(k, q)

        @block.scalar
        def _(act):
            act.dma_start(pad_rows[:, :], pad).then_inc(s_small, 16)
            act.dma_start(tok_ids[:, :], ids).then_inc(s_small, 16)
            act.dma_start(w_rel[:, :], W_rel).then_inc(s_small, 16)
            act.dma_start(w_root[:, :], W_root).then_inc(s_small, 16)
            act.dma_start(brel_row[0:1, :].rearrange("o (b c) -> o b c", b=UB),
                          b_rel[None, None, :].to_broadcast([1, UB, P])).then_inc(s_small, 16)
            act.dma_start(gam[:, :], gamma[:, None]).then_inc(s_small, 16)
            act.dma_start(bet[:, :], beta[:, None]).then_inc(s_small, 16)
            act.dma_start(wg[:, :], Wg).then_inc(s_small, 16)
            act.dma_start(bgb[:, :], bg[None, :].to_broadcast([P, E])).then_inc(s_exp, 16)
            act.dma_start(experts[:, :, 0:HID], W1.rearrange("e d h -> d e h")).then_inc(s_exp, 16)
            for k in range(HT):
                act.dma_start(experts[:, :, HID + k * P:HID + (k + 1) * P],
                              W2[:, k * P:(k + 1) * P, :].rearrange("e h d -> h e d")).then_inc(s_exp, 16)
                act.dma_start(experts[:, :, HID + HT * P + k], b1[:, k * P:(k + 1) * P].rearrange("e h -> h e"),
                              allow_slow_non_contiguous=True).then_inc(s_exp, 16)
            act.dma_start(b2b[:, :, :], b2[None, :, :].to_broadcast([P, E, P])).then_inc(s_exp, 16)
            act.wait_ge(s_small, 16 * SMALL)
            act.dma_start(rows_dram.bitcast(U32).rearrange("(g r) c -> g r c", g=NG)[:, 0:C, :]
                          .rearrange("g (p j) c -> p g (j c)", j=CJ),
                          pad_rows[:, None, :].to_broadcast([P, NG, CJ * ROW])).then_inc(s_pad, 16)

            def first(k, q):
                n, t = DEEP * k + q, q % 2
                act.wait_ge(s_psa, n + 1)
                if exists(k, q, 2, UNITS):
                    act.wait_ge(s_conv, n - 1)
                act.activation(aT[:, t], ps_a, ACT.Copy).then_inc(s_aT, 1)
                act.wait_ge(s_var1, n + 1)
                act.activation(std1[:, t], var1[:, t], ACT.Sqrt).then_inc(s_std1, 1)
                act.wait_ge(s_psz, n + 1)
                act.activation(hT[:, t], ps_z, ACT.Identity, bias=bet[:, :], scale=gam[:, :]).then_inc(s_hT, 1)
                act.wait_ge(s_coef, n + 1)
                if exists(k, q, 2, UNITS):
                    act.wait_ge(s_x1, n - 1)
                for b in range(UB):
                    last = act.activation(xr[:, t, b], xin[:, q, b], ACT.Identity, bias=xr_bias[:, t, b:b + 1],
                                          scale=xr_scale[:, t, b:b + 1])
                last.then_inc(s_xr, 1)
                act.wait_ge(s_psp, n + 1)
                act.activation(pr[:, t], ps_p, ACT.Copy).then_inc(s_pr, 1)

            def second(k, q):
                n, t = DEEP * k + q, q % 2
                act.wait_ge(s_var2, n + 1)
                act.activation(std2[:, t], var2[:, t], ACT.Sqrt).then_inc(s_std2, 1)
                act.wait_ge(s_psx, n + 1)
                if exists(k, q, 2, UNITS):
                    act.wait_ge(s_gate, n - 1)
                act.activation(xnT[:, t], ps_x, ACT.Copy).then_inc(s_xnT, 1)

            def slots(k):
                for q in range(DEEP):
                    if exists(k, q, 0, UNITS):
                        first(k, q)
                    if exists(k, q, 1, UNITS):
                        second(*back(k, q, 1))

            slots(0)
            with act.Fori(1, QUADS) as k:
                slots(k)
            slots(QUADS)

            def chunk_xT(k, q):
                n, t = DEEP * k + q, q % 2
                act.wait_ge(s_psxs, n + 1)
                if exists(k, q, 2, CHUNKS):
                    act.wait_ge(s_h, n - 1)
                act.activation(xsT[:, t], ps_xs[t], ACT.Copy).then_inc(s_xsT, 1)

            def gelus(k, q):
                n, t = DEEP * k + q, q % 2
                act.wait_ge(s_w, n + 1)
                act.wait_ge(s_h, n + 1)
                if exists(k, q, 2, CHUNKS):
                    act.wait_ge(s_y, n - 1)
                for s in range(2):
                    for h in range(HT):
                        last = act.activation(gT[:, t, s, h], ps_h[t][s][:, h], ACT.Gelu,
                                              bias=wbuf[:, q, s, HID + HT * P + h:HID + HT * P + h + 1])
                last.then_inc(s_gel, 1)

            def chunk_slots(k):
                for q in range(DEEP):
                    chunk_xT(k, q)
                    if exists(k, q, 1, CHUNKS):
                        gelus(*back(k, q, 1))

            chunk_slots(0)
            with act.Fori(1, CQUADS) as k:
                chunk_slots(k)
            gelus(*back(CQUADS, 0, 1))

        @block.vector
        def _(dve):
            dve.wait_ge(s_tab, 16)
            dve.wait_ge(s_ready, 4)
            dve.tensor_copy(tri[:, :], tab[:, T_TRI:T_TRI + P]).then_inc(s_setup, 1)
            dve.tensor_scalar(tri_rest[:, :], tab[:, T_TRI:T_TRI + P], -1.0, 1.0, ALU.mult, ALU.add)\
                .then_inc(s_setup, 1)
            dve.tensor_copy(base_row[:, :, :], tab[0:1, None, T_BASE:T_BASE + NG].to_broadcast([1, UB, NG]))\
                .then_inc(s_setup, 1)

            def ln1_stats(k, q):
                n, t = DEEP * k + q, q % 2
                dve.wait_ge(s_x[q], 16 * k + 16)
                for b in range(UB):
                    last = dve.bn_stats(st1[:, t, b], xin[:, q, b])
                last.then_inc(s_ln1, 1)
                dve.wait_ge(s_ln1, 3 * n + 1)
                dve.sem_inc(s_turn_dve, 1)
                for b in range(UB):
                    last = dve.bn_aggr(mv1[:, t, b], st1[:, t, b])
                last.then_inc(s_ln1, 1)
                dve.wait_ge(s_ln1, 3 * n + 2)
                dve.tensor_scalar(var1[:, t, 0], mv1[:, t, :, 1], EPS, None, ALU.add)
                dve.tensor_scalar(var1[:, t, 1], mv1[:, t, :, 1], 1.0 + EPS, EPS * EPS, ALU.mult, ALU.add)\
                    .then_inc(s_var1, 1)

            def ln1_apply(k, q):
                n, t = DEEP * k + q, q % 2
                dve.wait_ge(s_std1, n + 1)
                dve.reciprocal(rs1[:, t], std1[:, t]).then_inc(s_ln1, 1)
                dve.wait_ge(s_ln1, 3 * n + 3)
                dve.tensor_scalar(xr_scale[:, t], rs1[:, t, 0], 1.0, None, ALU.add)
                dve.scalar_tensor_tensor(xr_bias[:, t], mv1[:, t, :, 0], -1.0, rs1[:, t, 0], ALU.mult, ALU.mult)\
                    .then_inc(s_coef, 1)
                if exists(k, q, 2, UNITS):
                    dve.wait_ge(s_psz, n - 1)
                for b in range(UB):
                    last = dve.tensor_scalar(z[:, t, b], xin[:, q, b], mv1[:, t, b, 0:1], rs1[:, t, 1, b:b + 1],
                                             ALU.subtract, ALU.mult)
                last.then_inc(s_z, 1)

            def x1_stats(k, q):
                n, t = DEEP * k + q, q % 2
                dve.wait_ge(s_conv, n + 1)
                dve.wait_ge(s_xr, n + 1)
                if exists(k, q, DEEP, UNITS):
                    dve.wait_ge(s_scat[q], 16 * UB * k)
                dve.scalar_tensor_tensor(row[:, q, :, 0:P], ps_c[t], 0.0, xr[:, t], ALU.max, ALU.add)\
                    .then_inc(s_x1, 1)
                dve.wait_ge(s_x1, n + 1)
                for b in range(UB):
                    last = dve.bn_stats(st2[:, t, b], row[:, q, b, 0:P])
                last.then_inc(s_ln2, 1)
                dve.wait_ge(s_ln2, 2 * n + 1)
                dve.sem_inc(s_turn_dve, 1)
                for b in range(UB):
                    last = dve.bn_aggr(mv2[:, t, b], st2[:, t, b])
                last.then_inc(s_ln2, 1)
                dve.wait_ge(s_ln2, 2 * n + 2)
                dve.tensor_scalar(var2[:, t], mv2[:, t, :, 1], EPS, None, ALU.add).then_inc(s_var2, 1)
                dve.tensor_copy(row[:, q, :, MEAN], mv2[:, t, :, 0])

            def x1_norm(k, q):
                n, t = DEEP * k + q, q % 2
                dve.wait_ge(s_std2, n + 1)
                dve.reciprocal(row[:, q, :, RSTD], std2[:, t]).then_inc(s_rstd, 1)
                dve.wait_ge(s_rstd, n + 1)
                if exists(k, q, 2, UNITS):
                    dve.wait_ge(s_psx, n - 1)
                for b in range(UB):
                    last = dve.tensor_scalar(xn[:, t, b], row[:, q, b, 0:P], row[:, q, b, MEAN:MEAN + 1],
                                             row[:, q, b, RSTD:RSTD + 1], ALU.subtract, ALU.mult)
                last.then_inc(s_xn, 1)

            w_bc = tab[:, None, T_W:T_W + E].to_broadcast([P, UB, E])

            def top2(k, q):
                n, t = DEEP * k + q, q % 2
                STEPS = 12

                def step(i, ins):
                    ins.then_inc(s_top, 1)
                    dve.wait_ge(s_top, STEPS * n + i)

                def per_graph(v):
                    return v[:, :, None].to_broadcast([P, UB, E])

                dve.wait_ge(s_gate, n + 1)
                dve.tensor_tensor(g1[:, :, :], ps_g, bgb[:, None, :].to_broadcast([P, UB, E]), ALU.add)\
                    .then_inc(s_gread, 1)
                dve.wait_ge(s_gread, n + 1)
                step(1, dve.tensor_reduce(m1[:, :], g1[:, :, :], AX.X, ALU.max))
                step(2, dve.tensor_tensor(eq[:, :, :], g1[:, :, :], per_graph(m1), ALU.is_equal))
                step(3, dve.tensor_tensor(eqw[:, :, :], eq[:, :, :], w_bc, ALU.mult))
                step(4, dve.tensor_reduce(w1[:, :], eqw[:, :, :], AX.X, ALU.max))
                step(5, dve.tensor_tensor(eq[:, :, :], w_bc, per_graph(w1), ALU.is_equal))
                step(6, dve.scalar_tensor_tensor(g2[:, :, :], eq[:, :, :], -BIG, g1[:, :, :], ALU.mult, ALU.add))
                step(7, dve.tensor_reduce(m2[:, :], g2[:, :, :], AX.X, ALU.max))
                step(8, dve.tensor_tensor(eq[:, :, :], g2[:, :, :], per_graph(m2), ALU.is_equal))
                step(9, dve.tensor_tensor(eqw[:, :, :], eq[:, :, :], w_bc, ALU.mult))
                step(10, dve.tensor_reduce(w2[:, :], eqw[:, :, :], AX.X, ALU.max))
                dve.tensor_tensor(wx[:, :], w1[:, :], w2[:, :], ALU.max)
                step(11, dve.tensor_tensor(wn[:, :], w1[:, :], w2[:, :], ALU.min))
                step(12, dve.scalar_tensor_tensor(code[:, :], wx[:, :], float(E), wn[:, :], ALU.mult, ALU.add))
                if exists(k, q, 2, UNITS):
                    dve.wait_ge(s_cnt, n - 1)
                dve.tensor_tensor(onehot[:, t], tab[:, None, T_CODE:T_CODE + NG].to_broadcast([P, UB, NG]),
                                  code[:, :, None].to_broadcast([P, UB, NG]), ALU.is_equal).then_inc(s_hot, 1)

            def positions(k, q):
                n, t = DEEP * k + q, q % 2
                dve.wait_ge(s_rank, n + 1)
                dve.tensor_tensor(rank_m[:, :, :], ps_r, onehot[:, t], ALU.mult).then_inc(s_rread, 1)
                dve.wait_ge(s_rread, n + 1)
                with nc.allow_low_precision(reason="whole numbers below 2^24, summed in float32"):
                    dve.tensor_reduce(pos[:, q], rank_m[:, :, :], AX.X, ALU.add).then_inc(s_pos, 1)

            def slots(k):
                for q in range(DEEP):
                    if exists(k, q, 0, UNITS):
                        ln1_stats(k, q)
                    if exists(k, q, 2, UNITS):
                        top2(*back(k, q, 2))
                    if exists(k, q, 0, UNITS):
                        ln1_apply(k, q)
                    if exists(k, q, 1, UNITS):
                        x1_stats(*back(k, q, 1))
                    if exists(k, q, 2, UNITS):
                        positions(*back(k, q, 2))
                    if exists(k, q, 1, UNITS):
                        x1_norm(*back(k, q, 1))

            dve.wait_ge(s_exp, 16 * (3 + 2 * HT))
            g = 0
            for a in range(E - 1):
                n = E - 1 - a
                last = dve.tensor_tensor(b2_pair[:, g:g + n], b2b[:, a:a + 1].to_broadcast([P, n, P]),
                                         b2b[:, a + 1:E], ALU.add)
                g += n
            last.then_inc(s_b2, 1)
            slots(0)
            with dve.Fori(1, QUADS) as k:
                slots(k)
            slots(QUADS)

            STEPS = 0

            def step(ins):
                nonlocal STEPS
                STEPS += 1
                ins.then_inc(s_tb, 1)
                dve.wait_ge(s_tb, STEPS)

            base = tab[:, T_BASE:T_BASE + NG]
            chunk = tab[:, T_CHUNK:T_CHUNK + 1]
            vals = tab[:, T_VALS:T_VALS + 4 * NG].rearrange("p (v g) -> p v g", v=4)
            dve.wait_ge(s_cnt, UNITS)
            step(dve.tensor_tensor(cnt[:, :], ps_r[:, 0], base, ALU.subtract))
            step(dve.tensor_scalar(cnt_up[:, :], cnt[:, :], float(C - 1), None, ALU.add))
            step(dve.tensor_scalar(nch_i[:, :], cnt_up[:, :], C.bit_length() - 1, None, ALU.logical_shift_right))
            step(dve.tensor_copy(nch[:, :], nch_i[:, :]))
            step(dve.tensor_tensor_scan(c_end[:, :], nch[:, :], zero_g[:, :], 0.0, ALU.add, ALU.add))
            step(dve.tensor_tensor(c_beg[:, :], c_end[:, :], nch[:, :], ALU.subtract))
            dve.tensor_scalar(in_beg[:, :], c_beg[:, :], chunk, None, ALU.is_le)
            dve.tensor_scalar(in_end[:, :], c_end[:, :], chunk, None, ALU.is_gt)
            dve.tensor_scalar(at[:, :], c_beg[:, :], chunk, -float(C), ALU.subtract, ALU.mult)
            step(dve.tensor_scalar(last_at[:, :], cnt[:, :], -float(C), None, ALU.add))
            dve.tensor_tensor(in_g[:, :], in_beg[:, :], in_end[:, :], ALU.mult)
            step(dve.tensor_tensor(near[:, :], at[:, :], last_at[:, :], ALU.min))
            step(dve.tensor_tensor(vals[:, 0], near[:, :], base, ALU.add))
            step(dve.tensor_tensor(picked[:, :, :], vals, in_g[:, None, :].to_broadcast([P, 4, NG]), ALU.mult))
            with nc.allow_low_precision(reason="whole numbers below 2^24, summed in float32"):
                dve.tensor_reduce(chunk_cols[:, :], picked[:, :, :], AX.X, ALU.add).then_inc(s_tbd, 1)
            dve.wait_ge(s_tbm, 16)

            def value(n, v, top):
                return dve.value_load(chunk_tab[0:1, bass.ds(4 * n + v, 1)], min_val=0, max_val=top)

            def prepare(k, q):
                n, t = DEEP * k + q, q % 2
                if exists(k, q, DEEP, CHUNKS):
                    dve.wait_ge(s_y, n + 1 - DEEP)
                for s in range(2):
                    e = value(n, 1 + s, E - 1)
                    last = dve.tensor_copy(wbuf[:, q, s], experts[:, bass.ds(e, 1)].rearrange("p o c -> p (o c)"))
                last.then_inc(s_w, 1)
                dve.wait_ge(s_rows[q], 16 * k + 16)
                if exists(k, q, 2, CHUNKS):
                    dve.wait_ge(s_psxs, n - 1)
                for j in range(CJ):
                    last = dve.tensor_scalar(xs[:, t, j], rows[:, q, j, 0:P], rows[:, q, j, MEAN:MEAN + 1],
                                             rows[:, q, j, RSTD:RSTD + 1], ALU.subtract, ALU.mult)
                last.then_inc(s_xs, 1)
                g = value(n, 3, NG - 1)
                dve.tensor_tensor(xb[:, q], rows[:, q, :, 0:P],
                                  b2_pair[:, bass.ds(g, 1)].to_broadcast([P, CJ, P]), ALU.add).then_inc(s_xb, 1)

            def finish(k, q):
                n, t = DEEP * k + q, q % 2
                dve.wait_ge(s_y, n + 1)
                if exists(k, q, DEEP, CHUNKS):
                    dve.wait_ge(s_out[q], 16 * CJ * k)
                dve.wait_ge(s_xb, n + 1)
                dve.tensor_tensor(ob[:, q], ps_y[t], xb[:, q], ALU.add).then_inc(s_ob, 1)

            def chunk_slots(k):
                for q in range(DEEP):
                    if exists(k, q, 0, CHUNKS):
                        prepare(k, q)
                    if exists(k, q, 3, CHUNKS):
                        finish(*back(k, q, 3))

            chunk_slots(0)
            with dve.Fori(1, CQUADS) as k:
                chunk_slots(k)
            chunk_slots(CQUADS)

        @block.tensor
        def _(pe):
            def transposes(k, q):
                n, t = DEEP * k + q, q % 2
                pe.wait_ge(s_adj[q], 16 * k + 16)
                if exists(k, q, 1, UNITS):
                    pe.wait_ge(s_aT, n)
                for b in range(UB):
                    last = pe.transpose(ps_a[:, b], ain[:, q, b], ident)
                last.then_inc(s_psa, 1)
                pe.wait_ge(s_z, n + 1)
                if exists(k, q, 1, UNITS):
                    pe.wait_ge(s_hT, n)
                for b in range(UB):
                    last = pe.transpose(ps_z[:, b], z[:, t, b], ident)
                last.then_inc(s_psz, 1)

            def gnn(k, q):
                n, t = DEEP * k + q, q % 2
                if exists(k, q, 2, UNITS):
                    pe.wait_ge(s_x1, n - 1)
                pe.matmul(ps_c[t], ones_row[:, :], brel_row[:, :], start=True, stop=False,
                          skip_group_check=True)
                pe.wait_ge(s_hT, n + 1)
                if exists(k, q, 1, UNITS):
                    pe.wait_ge(s_pr, n)
                for b in range(UB):
                    last = pe.matmul(ps_p[:, b], hT[:, t, b], w_rel[:, :], start=True, stop=True)
                last.then_inc(s_psp, 1)
                for b in range(UB):
                    pe.matmul(ps_c[t][:, b], hT[:, t, b], w_root[:, :], start=False, stop=False,
                              skip_group_check=True)
                pe.wait_ge(s_aT, n + 1)
                pe.wait_ge(s_pr, n + 1)
                for b in range(UB):
                    last = pe.matmul(ps_c[t][:, b], aT[:, t, b], pr[:, t, b], start=False, stop=b == UB - 1,
                                     skip_group_check=True)
                last.then_inc(s_conv, 1)

            def gates(k, q):
                n, t = DEEP * k + q, q % 2
                pe.wait_ge(s_xn, n + 1)
                if exists(k, q, 1, UNITS):
                    pe.wait_ge(s_xnT, n)
                for b in range(UB):
                    last = pe.transpose(ps_x[:, b], xn[:, t, b], ident)
                last.then_inc(s_psx, 1)
                pe.wait_ge(s_xnT, n + 1)
                if exists(k, q, 1, UNITS):
                    pe.wait_ge(s_gread, n)
                for b in range(UB):
                    last = pe.matmul(ps_g[:, b], xnT[:, t, b], wg[:, :], start=True, stop=True)
                last.then_inc(s_gate, 1)

            def ranks(k, q):
                n, t = DEEP * k + q, q % 2
                pe.wait_ge(s_hot, n + 1)
                last = pe.matmul(ps_r, tri[:, :], onehot[:, t], start=False, stop=False, skip_group_check=True)
                for b in range(UB - 1):
                    m = UB - 1 - b
                    last = pe.matmul(ps_r[:, b + 1:UB], ones[:, :],
                                     onehot[:, t, b:b + 1].to_broadcast([P, m, NG]),
                                     start=False, stop=False, skip_group_check=True)
                last.then_inc(s_rank, 1)

            def counts(k, q):
                n, t = DEEP * k + q, q % 2
                pe.wait_ge(s_rread, n + 1)
                pe.matmul(ps_r, tri_rest[:, :], onehot[:, t], start=False, stop=False, skip_group_check=True)
                for b in range(1, UB):
                    last = pe.matmul(ps_r[:, 0:b], ones[:, :], onehot[:, t, b:b + 1].to_broadcast([P, b, NG]),
                                     start=False, stop=False, skip_group_check=True)
                last.then_inc(s_cnt, 1)

            def slots(k):
                for q in range(DEEP):
                    if exists(k, q, 0, UNITS):
                        transposes(k, q)
                    if exists(k, q, 2, UNITS):
                        ranks(*back(k, q, 2))
                    if exists(k, q, 0, UNITS):
                        gnn(k, q)
                    if exists(k, q, 2, UNITS):
                        counts(*back(k, q, 2))
                    if exists(k, q, 1, UNITS):
                        gates(*back(k, q, 1))

            pe.wait_ge(s_tab, 16)
            pe.wait_ge(s_ready, 4)
            pe.wait_ge(s_setup, 3)
            pe.wait_ge(s_small, 16 * SMALL)
            pe.matmul(ps_r, ones_row[:, :], base_row[:, :, :], start=True, stop=False, skip_group_check=True)
            slots(0)
            with pe.Fori(1, QUADS) as k:
                slots(k)
            slots(QUADS)

            def chunk_transpose(k, q):
                n, t = DEEP * k + q, q % 2
                pe.wait_ge(s_xs, n + 1)
                if exists(k, q, 2, CHUNKS):
                    pe.wait_ge(s_xsT, n - 1)
                for j in range(CJ):
                    last = pe.transpose(ps_xs[t][:, j * P:(j + 1) * P], xs[:, t, j], ident)
                last.then_inc(s_psxs, 1)

            def up(k, q):
                n, t = DEEP * k + q, q % 2
                pe.wait_ge(s_w, n + 1)
                pe.wait_ge(s_xsT, n + 1)
                if exists(k, q, 2, CHUNKS):
                    pe.wait_ge(s_gel, n - 1)
                for s in range(2):
                    for h in range(HT):
                        last = pe.matmul(ps_h[t][s][:, h], wbuf[:, q, s, h * P:(h + 1) * P], xsT[:, t],
                                         start=True, stop=True)
                last.then_inc(s_h, 1)

            def down(k, q):
                n, t = DEEP * k + q, q % 2
                pe.wait_ge(s_gel, n + 1)
                if exists(k, q, 2, CHUNKS):
                    pe.wait_ge(s_ob, n - 1)
                for j in range(CJ):
                    for s in range(2):
                        for h in range(HT):
                            last = pe.matmul(ps_y[t][:, j], gT[:, t, s, h, j * P:(j + 1) * P],
                                             wbuf[:, q, s, HID + h * P:HID + (h + 1) * P],
                                             start=s + h == 0, stop=s + h == HT)
                last.then_inc(s_y, 1)

            def chunk_slots(k):
                for q in range(DEEP):
                    if exists(k, q, 0, CHUNKS):
                        chunk_transpose(k, q)
                    if exists(k, q, 1, CHUNKS):
                        up(*back(k, q, 1))
                    if exists(k, q, 2, CHUNKS):
                        down(*back(k, q, 2))

            chunk_slots(0)
            with pe.Fori(1, CQUADS) as k:
                chunk_slots(k)
            chunk_slots(CQUADS)


INPUTS = ["x", "adj", "L0_gnn_W_rel", "L0_gnn_b_rel", "L0_gnn_W_root", "L0_gnn_ln_gamma", "L0_gnn_ln_beta",
          "L0_ffn_Wg", "L0_ffn_bg", "L0_ffn_W1", "L0_ffn_b1", "L0_ffn_W2", "L0_ffn_b2"]


def kernel(**inputs):
    import numpy as _np
    import concourse.bacc as _bacc
    from concourse import mybir as _mybir
    from concourse.bass_utils import run_bass_kernel_spmd as _run

    nc = _bacc.Bacc("TRN2", target_bir_lowering=False, num_devices=1)
    arrays, args = {}, []
    named = [(n, _np.ascontiguousarray(inputs[n])) for n in INPUTS]
    named += list(zip(["shape_table", "token_ids", "padding_rows"], constants()))
    for name, a in named:
        arrays[f"in_{name}"] = a
        args.append(nc.dram_tensor(f"in_{name}", a.shape, _mybir.dt.from_np(a.dtype), kind="ExternalInput").ap())
    out = nc.dram_tensor("out_rows", (TOKENS, P), _mybir.dt.float32, kind="ExternalOutput").ap()
    build(nc, *args, out)
    r = _run(nc, [arrays], core_ids=[0])
    return r.results[0]["out_rows"].reshape(GRAPHS, P, P)
```

```python
from contextlib import ExitStack

import numpy as np

import concourse.bass as bass
from concourse import mybir

F32 = mybir.dt.float32
BF16 = mybir.dt.bfloat16
U32 = mybir.dt.uint32
I32 = mybir.dt.int32
ALU = mybir.AluOpType
ACT = mybir.ActivationFunctionType
AX = mybir.AxisListType

P = 128
GRAPHS = 128
TOKENS = GRAPHS * P
UB = 4
UNITS = GRAPHS // UB
A_DEEP = 8
A_LOOPS = UNITS // A_DEEP
LOADS = 4
DEEP = 4
E = 8
HID = 256
HT = HID // P
EPS = 1e-5
PAIRS = [(a, b) for a in range(E) for b in range(a + 1, E)]
NG = len(PAIRS)
C = 256
CJ = C // P
REGION = C + TOKENS
CHUNKS = (TOKENS - NG) // C + NG
CHUNKS += -CHUNKS % DEEP
CQUADS = CHUNKS // DEEP
ROW = 132
ID, MEAN, RSTD = P, P + 1, P + 2
PACK = HID + HT * P + HT
BIG = 1e38

T_IDENT = 0
T_TRI = T_IDENT + P
T_W = T_TRI + P
T_CODE = T_W + E
T_BASE = T_CODE + NG
T_VALS = T_BASE + NG
T_CHUNK = T_VALS + 4 * NG
T_COLS = T_CHUNK + 1


def constants():
    t = np.zeros((P, T_COLS), np.float32)
    t[:, T_IDENT:T_IDENT + P] = np.eye(P)
    t[:, T_TRI:T_TRI + P] = np.triu(np.ones((P, P)), 1)
    t[:, T_W:T_W + E] = E - np.arange(E)
    t[:, T_CODE:T_CODE + NG] = [(E - a) * E + (E - b) for a, b in PAIRS]
    t[:, T_BASE:T_BASE + NG] = [g * REGION + C for g in range(NG)]
    t[:, T_VALS + NG:T_VALS + 2 * NG] = [a for a, b in PAIRS]
    t[:, T_VALS + 2 * NG:T_VALS + 3 * NG] = [b for a, b in PAIRS]
    t[:, T_VALS + 3 * NG:T_VALS + 4 * NG] = np.arange(NG)
    t[:, T_CHUNK] = np.arange(P)
    ids = (np.arange(P)[:, None] + P * np.arange(GRAPHS)[None, :]).astype(np.uint32)
    pad = np.zeros((P, CJ * ROW), np.uint32)
    pad[:, ID::ROW] = TOKENS
    return t, ids, pad


def back(k, q, d, deep):
    return (k, q - d) if q >= d else (k - 1, q - d + deep)


def exists(k, q, d, deep, n):
    return not isinstance(k, int) or 0 <= deep * k + q - d < n


def unit(k, q, d=0):
    return exists(k, q, d, A_DEEP, UNITS)


def slot(k, q, d=0):
    return exists(k, q, d, A_DEEP, UNITS + 2)


def chunk(k, q, d=0):
    return exists(k, q, d, DEEP, CHUNKS)


def build(nc, x, adj, W_rel, b_rel, W_root, gamma, beta, Wg, bg, W1, b1, W2, b2, table, ids, pad, out):
    rows_dram = nc.dram_tensor("rows_by_group", [NG * REGION, ROW], F32, kind="Internal").ap()

    with ExitStack() as ctx:
        def sb(name, shape, dt=F32):
            return ctx.enter_context(nc.sbuf_tensor(name, shape, dt))

        def sem(name):
            return ctx.enter_context(nc.semaphore(name))

        def sems(name, n):
            return [sem(f"{name}{i}") for i in range(n)]

        tab = sb("tab", [P, T_COLS])
        ident = tab[:, T_IDENT:T_IDENT + P]
        tok_ids = sb("tok_ids", [P, GRAPHS], U32)
        pad_rows = sb("pad_rows", [P, CJ * ROW], U32)
        tri = sb("tri", [P, P], BF16)
        tri_rest = sb("tri_rest", [P, P], BF16)
        ones = sb("ones", [P, P], BF16)
        ones_row = sb("ones_row", [1, P])
        base_row = sb("base_row", [1, 2 * UB, NG])
        w_in = sb("w_in", [P, 2, P])
        w_gam = sb("w_gam", [P, 2, P])
        w_cen = sb("w_cen", [P, 2, P])
        center = sb("center", [P, P])
        gam = sb("gam", [P, 1])
        bet = sb("bet", [P, 1])
        bet_mat = sb("bet_mat", [P, P])
        brel_b = sb("brel_b", [P, P])
        const_b = sb("const_b", [P, 2, P])
        wg_in = sb("wg_in", [P, E])
        wg = sb("wg", [P, E])
        bgb = sb("bgb", [P, E])
        experts = sb("experts", [P, E, PACK])
        b2b = sb("b2b", [P, E, P])
        b2_pair = sb("b2_pair", [P, NG, P])

        xin = sb("xin", [P, LOADS, UB, P])
        ain = sb("ain", [P, LOADS, UB, P])
        st = sb("st", [P, 2, 2, UB, 6])
        mv = sb("mv", [P, 2, 2, UB, 2])
        var = sb("var", [P, 2, 3, UB])
        std = sb("std", [P, 2, 3, UB])
        rstd = sb("rstd", [P, 2, 3, UB])
        xr_scale = sb("xr_scale", [P, 2, UB])
        xr_bias = sb("xr_bias", [P, 2, UB])
        xT = sb("xT", [P, 2, UB, P])
        aT = sb("aT", [P, 2, UB, P])
        pr = sb("pr", [P, 2, UB, 2, P])
        xr = sb("xr", [P, 2, UB, P])
        row = sb("row", [P, A_DEEP, UB, ROW])
        row_u = row[:, :, :, :].bitcast(U32)
        x1T = sb("x1T", [P, 2, UB, P])
        PB = 2 * UB
        gx = sb("gx", [P, PB, E])
        g1 = sb("g1", [P, PB, E])
        g2 = sb("g2", [P, PB, E])
        eq = sb("eq", [P, PB, E])
        eqw = sb("eqw", [P, PB, E])
        m1 = sb("m1", [P, PB])
        m2 = sb("m2", [P, PB])
        w1 = sb("w1", [P, PB])
        w2 = sb("w2", [P, PB])
        wx = sb("wx", [P, PB])
        wn = sb("wn", [P, PB])
        code = sb("code", [P, PB])
        onehot = sb("onehot", [P, PB, NG], BF16)
        rank_m = sb("rank_m", [P, PB, NG])
        pos = sb("pos", [P, 4, PB], U32)

        cnt = sb("cnt", [P, NG])
        cnt_up = sb("cnt_up", [P, NG], I32)
        nch_i = sb("nch_i", [P, NG], I32)
        nch = sb("nch", [P, NG])
        zero_g = sb("zero_g", [P, NG])
        c_end = sb("c_end", [P, NG])
        c_beg = sb("c_beg", [P, NG])
        in_beg = sb("in_beg", [P, NG])
        in_end = sb("in_end", [P, NG])
        in_g = sb("in_g", [P, NG])
        at = sb("at", [P, NG])
        last_at = sb("last_at", [P, NG])
        near = sb("near", [P, NG])
        picked = sb("picked", [P, 4, NG])
        chunk_cols = sb("chunk_cols", [P, 4], I32)
        chunk_tab = sb("chunk_tab", [1, CHUNKS * 4], I32)

        rows = sb("rows", [P, DEEP, CJ, ROW])
        rows_u = rows[:, :, :, :].bitcast(U32)
        out_ids = sb("out_ids", [P, DEEP, CJ], U32)
        wbuf = sb("wbuf", [P, DEEP, 2, PACK])
        xs = sb("xs", [P, 2, CJ, P])
        xsT = sb("xsT", [P, 2, C])
        xb = sb("xb", [P, DEEP, CJ, P])
        gT = sb("gT", [P, 2, 2, HT, C])
        ob = sb("ob", [P, DEEP, CJ, P])

        bank = [ctx.enter_context(nc.psum_tensor(f"bank{i}", [P, 512], F32)) for i in range(8)]

        def four(b):
            return b[:, :].rearrange("p (b c) -> p b c", b=UB)

        ps_a, ps_x, ps_c, ps_x1 = four(bank[0]), four(bank[1]), four(bank[2]), four(bank[3])
        ps_pr = [bank[4 + i][:, :].rearrange("p (b w c) -> p b w c", b=2, w=2) for i in range(2)]
        ps_g = bank[6][:, 0:PB * E].rearrange("p (b e) -> p b e", b=PB)
        ps_r = bank[7][:, 0:PB * NG].rearrange("p (b g) -> p b g", b=PB)
        ps_w = bank[4][:, 0:2 * P].rearrange("p (w c) -> p w c", w=2)
        ps_cb = bank[5][:, 0:2 * P].rearrange("p (w c) -> p w c", w=2)
        ps_wg = bank[6][:, 0:E]
        ps_xs = [bank[0][:, 0:C], bank[7][:, 0:C]]
        ps_h = [[bank[1 + 2 * t + s][:, :].rearrange("p (k c) -> p k c", k=HT) for s in range(2)] for t in range(2)]
        ps_y = [bank[5 + t][:, 0:C].rearrange("p (j c) -> p j c", j=CJ) for t in range(2)]

        s_tab = sem("tables_in")
        s_small = sem("small_weights_in")
        s_exp = sem("experts_in")
        s_pad = sem("padding_rows_out")
        s_ready = sem("constants_built")
        s_setup = sem("setup_step")
        s_b2 = sem("b2_pairs_built")
        s_fold = sem("folded_weights_in_psum")
        s_x = sems("x_in", LOADS)
        s_adj = sems("adj_in", LOADS)
        s_psa = sem("adjT_in_psum")
        s_aT = sem("adjT_ready")
        s_psxT = sem("xT_in_psum")
        s_xT = sem("xT_ready")
        s_pspr = sem("products_in_psum")
        s_pr = sem("products_ready")
        s_conv = sem("conv_in_psum")
        s_bn = sem("bn_step")
        s_var = sem("variances_ready")
        s_std = sem("stds_ready")
        s_rstd = sem("rstds_ready")
        s_coef = sem("residual_coefs_ready")
        s_xr = sem("residual_ready")
        s_x1 = sem("x1_ready")
        s_meta = sem("row_stats_ready")
        s_psx1 = sem("x1T_in_psum")
        s_x1T = sem("x1T_ready")
        s_gate = sem("gates_in_psum")
        s_top = sem("top2_step")
        s_gread = sem("gates_read")
        s_hot = sem("onehot_ready")
        s_rank = sem("ranks_in_psum")
        s_rread = sem("ranks_read")
        s_cnt = sem("counts_in_psum")
        s_pos = sem("positions_ready")
        s_rid = sem("row_ids_ready")
        s_scat = sems("rows_scattered", A_DEEP)
        s_tb = sem("chunk_table_step")
        s_tbd = sem("chunk_table_ready")
        s_tbm = sem("chunk_table_in_row")
        s_rows = sems("rows_in", DEEP)
        s_w = sem("weights_copied")
        s_xs = sem("chunk_normed")
        s_xb = sem("rows_used")
        s_psxs = sem("chunk_xT_in_psum")
        s_xsT = sem("chunk_xT_ready")
        s_h = sem("hidden_in_psum")
        s_gel = sem("gelu_ready")
        s_y = sem("y_in_psum")
        s_ob = sem("out_rows_ready")
        s_out = sems("out_rows_scattered", DEEP)

        s_turn_pool = sem("pool_wait_done")
        s_turn_dve = sem("dve_wait_done")

        SMALL = 8
        block = ctx.enter_context(nc.Block())

        @block.sync
        def _(sp):
            sp.dma_start(tab[:, :], table).then_inc(s_tab, 16)

            def load(k, q):
                m, n = q % LOADS, A_DEEP * k + q
                if unit(k, q, LOADS):
                    sp.wait_ge(s_xr, n + 1 - LOADS)
                    sp.wait_ge(s_psxT, n + 1 - LOADS)
                sp.dma_start(xin[:, m], x[bass.ds(UB * A_DEEP * k + UB * q, UB)].rearrange("b p c -> p b c"))\
                    .then_inc(s_x[m], 16)
                sp.dma_start(ain[:, m], adj[bass.ds(UB * A_DEEP * k + UB * q, UB)].rearrange("b p c -> p b c"))\
                    .then_inc(s_adj[m], 16)

            for q in range(A_DEEP):
                load(0, q)
            with sp.Fori(1, A_LOOPS) as k:
                for q in range(A_DEEP):
                    load(k, q)

            sp.wait_ge(s_tbd, 1)
            sp.dma_start(chunk_tab[0:1, :].rearrange("o (c v) -> o c v", v=4), chunk_cols[0:CHUNKS, :])\
                .then_inc(s_tbm, 16)
            sp.wait_ge(s_tbm, 16)
            sp.wait_ge(s_pad, 16)
            for q in range(A_DEEP):
                sp.wait_ge(s_scat[q], 16 * UB * A_LOOPS)

            def load_rows(k, q):
                if chunk(k, q, DEEP):
                    sp.wait_ge(s_xb, DEEP * (k - 1) + q + 1)
                first = sp.value_load(chunk_tab[0:1, bass.ds(4 * (DEEP * k + q), 1)], min_val=0,
                                      max_val=NG * REGION - C)
                sp.dma_start(rows[:, q], rows_dram[bass.ds(first, C)].rearrange("(p j) c -> p j c", j=CJ))\
                    .then_inc(s_rows[q], 16)

            for q in range(DEEP):
                load_rows(0, q)
            with sp.Fori(1, CQUADS) as k:
                for q in range(DEEP):
                    load_rows(k, q)
            for q in range(DEEP):
                sp.wait_ge(s_out[q], 16 * CJ * CQUADS)

        @block.gpsimd
        def _(pool):
            pool.memset(ones[:, :], 1.0).then_inc(s_ready, 1)
            pool.memset(ones_row[:, :], 1.0).then_inc(s_ready, 1)
            pool.memset(zero_g[:, :], 0.0).then_inc(s_ready, 1)
            pool.memset(row[:, :, :, RSTD + 1:ROW], 0.0).then_inc(s_ready, 1)
            pool.memset(mv[:, :, :, :, :], 1.0).then_inc(s_ready, 1)
            pool.wait_ge(s_small, 16 * SMALL)

            def scatter(k, q):
                n, pair = A_DEEP * k + q, A_DEEP // 2 * k + q // 2
                if unit(k, q, A_DEEP):
                    pool.wait_ge(s_scat[q], 16 * UB * k)
                pool.sem_inc(s_turn_pool, 1)
                pool.tensor_copy(row_u[:, q, :, ID], tok_ids[:, bass.ds(UB * A_DEEP * k + UB * q, UB)])\
                    .then_inc(s_rid, 1)
                pool.wait_ge(s_rid, n + 1)
                pool.wait_ge(s_meta, n + 1)
                pool.wait_ge(s_pos, pair + 1)
                pool.sem_inc(s_turn_pool, 1)
                for b in range(UB):
                    g = UB * (q % 2) + b
                    pool.indirect_dma_start(rows_dram,
                                            bass.IndirectOffsetOnAxis(ap=pos[:, q // 2, g:g + 1], axis=0),
                                            row[:, q, b], None).then_inc(s_scat[q], 16)

            for q in range(A_DEEP):
                scatter(0, q)
            with pool.Fori(1, A_LOOPS) as k:
                for q in range(A_DEEP):
                    scatter(k, q)

            def scatter_out(k, q):
                pool.wait_ge(s_ob, DEEP * k + q + 1)
                pool.sem_inc(s_turn_pool, 1)
                for j in range(CJ):
                    pool.indirect_dma_start(out, bass.IndirectOffsetOnAxis(ap=out_ids[:, q, j:j + 1], axis=0),
                                            ob[:, q, j], None, bounds_check=TOKENS - 1, oob_is_err=False)\
                        .then_inc(s_out[q], 16)

            with pool.Fori(0, CQUADS) as k:
                for q in range(DEEP):
                    scatter_out(k, q)

        @block.scalar
        def _(act):
            act.dma_start(pad_rows[:, :], pad).then_inc(s_small, 16)
            act.dma_start(tok_ids[:, :], ids).then_inc(s_small, 16)
            act.dma_start(w_in[:, 0], W_rel).then_inc(s_small, 16)
            act.dma_start(w_in[:, 1], W_root).then_inc(s_small, 16)
            act.dma_start(brel_b[:, :], b_rel[None, :].to_broadcast([P, P])).then_inc(s_small, 16)
            act.dma_start(gam[:, :], gamma[:, None]).then_inc(s_small, 16)
            act.dma_start(bet[:, :], beta[:, None]).then_inc(s_small, 16)
            act.dma_start(wg_in[:, :], Wg).then_inc(s_small, 16)
            act.dma_start(bgb[:, :], bg[None, :].to_broadcast([P, E])).then_inc(s_exp, 16)
            act.dma_start(experts[:, :, 0:HID], W1.rearrange("e d h -> d e h")).then_inc(s_exp, 16)
            for k in range(HT):
                act.dma_start(experts[:, :, HID + k * P:HID + (k + 1) * P],
                              W2[:, k * P:(k + 1) * P, :].rearrange("e h d -> h e d")).then_inc(s_exp, 16)
                act.dma_start(experts[:, :, HID + HT * P + k], b1[:, k * P:(k + 1) * P].rearrange("e h -> h e"),
                              allow_slow_non_contiguous=True).then_inc(s_exp, 16)
            act.dma_start(b2b[:, :, :], b2[None, :, :].to_broadcast([P, E, P])).then_inc(s_exp, 16)
            act.wait_ge(s_small, 16 * SMALL)
            act.dma_start(rows_dram.bitcast(U32).rearrange("(g r) c -> g r c", g=NG)[:, 0:C, :]
                          .rearrange("g (p j) c -> p g (j c)", j=CJ),
                          pad_rows[:, None, :].to_broadcast([P, NG, CJ * ROW])).then_inc(s_pad, 16)

            def transposed(k, q):
                n, t = A_DEEP * k + q, q % 2
                act.wait_ge(s_psa, n + 1)
                if unit(k, q, 2):
                    act.wait_ge(s_conv, n - 1)
                act.activation(aT[:, t], ps_a, ACT.Copy).then_inc(s_aT, 1)
                act.wait_ge(s_psxT, n + 1)
                if unit(k, q, 2):
                    act.wait_ge(s_pspr, n - 1)
                act.activation(xT[:, t], ps_x, ACT.Copy).then_inc(s_xT, 1)

            def x1_transposed(k, q):
                n, t = A_DEEP * k + q, q % 2
                act.wait_ge(s_psx1, n + 1)
                if unit(k, q, 2):
                    act.wait_ge(s_gate, n - 1)
                act.activation(x1T[:, t], ps_x1, ACT.Copy).then_inc(s_x1T, 1)

            def residual(k, q):
                n, t = A_DEEP * k + q, q % 2
                act.wait_ge(s_coef, n + 1)
                if unit(k, q, 2):
                    act.wait_ge(s_x1, n - 1)
                for b in range(UB):
                    last = act.activation(xr[:, t, b], xin[:, q % LOADS, b], ACT.Identity,
                                          bias=xr_bias[:, t, b:b + 1], scale=xr_scale[:, t, b:b + 1])
                last.then_inc(s_xr, 1)

            def row_stats(k, q):
                n, t = A_DEEP * k + q, q % 2
                act.wait_ge(s_rstd, n + 3)
                if unit(k, q, A_DEEP):
                    act.wait_ge(s_scat[q], 16 * UB * k)
                act.activation(row[:, q, :, MEAN], mv[:, t, 1, :, 0], ACT.Copy)
                act.activation(row[:, q, :, RSTD], rstd[:, t, 1], ACT.Copy).then_inc(s_meta, 1)

            def stds(k, q):
                n, t = A_DEEP * k + q, q % 2
                act.wait_ge(s_var, n + 1)
                act.activation(std[:, t], var[:, t], ACT.Sqrt).then_inc(s_std, 1)

            def slots(k):
                for q in range(A_DEEP):
                    if unit(k, q):
                        transposed(k, q)
                    if unit(k, q, 2):
                        x1_transposed(*back(k, q, 2, A_DEEP))
                    if unit(k, q, 1):
                        residual(*back(k, q, 1, A_DEEP))
                    if unit(k, q, 3):
                        row_stats(*back(k, q, 3, A_DEEP))
                    if slot(k, q):
                        stds(k, q)

            slots(0)
            with act.Fori(1, A_LOOPS) as k:
                slots(k)
            slots(A_LOOPS)

            def chunk_xT(k, q):
                n, t = DEEP * k + q, q % 2
                act.wait_ge(s_psxs, n + 1)
                if chunk(k, q, 2):
                    act.wait_ge(s_h, n - 1)
                act.activation(xsT[:, t], ps_xs[t], ACT.Copy).then_inc(s_xsT, 1)

            def gelus(k, q):
                n, t = DEEP * k + q, q % 2
                act.wait_ge(s_w, n + 1)
                act.wait_ge(s_h, n + 1)
                if chunk(k, q, 2):
                    act.wait_ge(s_y, n - 1)
                for s in range(2):
                    for h in range(HT):
                        last = act.activation(gT[:, t, s, h], ps_h[t][s][:, h], ACT.Gelu,
                                              bias=wbuf[:, q, s, HID + HT * P + h:HID + HT * P + h + 1])
                last.then_inc(s_gel, 1)

            def chunk_slots(k):
                for q in range(DEEP):
                    chunk_xT(k, q)
                    if chunk(k, q, 1):
                        gelus(*back(k, q, 1, DEEP))

            chunk_slots(0)
            with act.Fori(1, CQUADS) as k:
                chunk_slots(k)
            gelus(*back(CQUADS, 0, 1, DEEP))

        @block.vector
        def _(dve):
            dve.wait_ge(s_tab, 16)
            dve.wait_ge(s_ready, 5)
            dve.tensor_copy(tri[:, :], tab[:, T_TRI:T_TRI + P]).then_inc(s_setup, 1)
            dve.tensor_scalar(tri_rest[:, :], tab[:, T_TRI:T_TRI + P], -1.0, 1.0, ALU.mult, ALU.add)\
                .then_inc(s_setup, 1)
            dve.tensor_copy(base_row[:, :, :], tab[0:1, None, T_BASE:T_BASE + NG].to_broadcast([1, PB, NG]))\
                .then_inc(s_setup, 1)
            dve.tensor_scalar(center[:, :], ident, -1.0 / P, None, ALU.add).then_inc(s_setup, 1)
            dve.wait_ge(s_small, 16 * SMALL)
            dve.tensor_scalar(w_gam[:, :, :], w_in[:, :, :], gam[:, :], None, ALU.mult).then_inc(s_setup, 1)
            dve.tensor_copy(bet_mat[:, :], bet[:, :].to_broadcast([P, P])).then_inc(s_setup, 1)
            dve.wait_ge(s_fold, 1)
            dve.tensor_copy(w_cen[:, :, :], ps_w).then_inc(s_setup, 1)
            dve.tensor_copy(const_b[:, 0], ps_cb[:, 0]).then_inc(s_setup, 1)
            dve.tensor_tensor(const_b[:, 1], ps_cb[:, 1], brel_b[:, :], ALU.add).then_inc(s_setup, 1)
            dve.tensor_copy(wg[:, :], ps_wg).then_inc(s_setup, 1)

            w_bc = tab[:, None, T_W:T_W + E].to_broadcast([P, PB, E])

            def x1(k, q):
                n, t = A_DEEP * k + q, q % 2
                dve.wait_ge(s_conv, n + 1)
                dve.wait_ge(s_xr, n + 1)
                if unit(k, q, A_DEEP):
                    dve.wait_ge(s_scat[q], 16 * UB * k)
                dve.scalar_tensor_tensor(row[:, q, :, 0:P], ps_c, 0.0, xr[:, t], ALU.max, ALU.add)\
                    .then_inc(s_x1, 1)

            def rstds(k, q):
                n, t = A_DEEP * k + q, q % 2
                dve.wait_ge(s_std, n + 1)
                dve.reciprocal(rstd[:, t], std[:, t]).then_inc(s_rstd, 1)

            def coefs(k, q):
                n, t = A_DEEP * k + q, q % 2
                dve.wait_ge(s_rstd, n + 1)
                dve.tensor_scalar(xr_scale[:, t], rstd[:, t, 0], 1.0, None, ALU.add)
                dve.scalar_tensor_tensor(xr_bias[:, t], mv[:, t, 0, :, 0], -1.0, rstd[:, t, 0], ALU.mult, ALU.mult)\
                    .then_inc(s_coef, 1)

            def product(k, q, b):
                n, t = A_DEEP * k + q, q % 2
                if b == 0:
                    dve.wait_ge(s_pspr, n + 1)
                    if unit(k, q, 2):
                        dve.wait_ge(s_conv, n - 1)
                last = dve.scalar_tensor_tensor(pr[:, t, b], ps_pr[b // 2][:, b % 2], rstd[:, t, 2, b:b + 1],
                                                const_b[:, :, :], ALU.mult, ALU.add)
                if b == UB - 1:
                    last.then_inc(s_pr, 1)

            def stats1(k, q, b):
                if b == 0:
                    m = q % LOADS
                    dve.wait_ge(s_x[m], 16 * (A_DEEP // LOADS * k + q // LOADS + 1))
                return dve.bn_stats(st[:, q % 2, 0, b], xin[:, q % LOADS, b])

            def stats2(k, q, b):
                u = (q - 2) % A_DEEP
                if b == 0:
                    dve.wait_ge(s_x1, A_DEEP * k + q - 1)
                return dve.bn_stats(st[:, q % 2, 1, b], row[:, u, b, 0:P])

            def aggregate(k, q, w, b):
                return dve.bn_aggr(mv[:, q % 2, w, b], st[:, q % 2, w, b])

            def variances(k, q):
                n, t = A_DEEP * k + q, q % 2
                dve.wait_ge(s_bn, 2 * n + 2)
                dve.tensor_scalar(var[:, t, 0:2], mv[:, t, :, :, 1], EPS, None, ALU.add)
                dve.tensor_scalar(var[:, t, 2], mv[:, t, 0, :, 1], 1.0 + EPS, EPS * EPS, ALU.mult, ALU.add)\
                    .then_inc(s_var, 1)

            TOP_STEPS = 13

            def top2(pair):

                def per_graph(v):
                    return v[:, :, None].to_broadcast([P, PB, E])

                base = TOP_STEPS * pair

                def after(i):
                    dve.wait_ge(s_top, base + i)

                dve.wait_ge(s_gate, 2 * pair + 2)
                dve.wait_ge(s_rstd, 2 * pair + 4)
                dve.tensor_tensor(gx[:, :, :].rearrange("p (t b) e -> p t b e", t=2),
                                  ps_g.rearrange("p (t b) e -> p t b e", t=2),
                                  rstd[:, :, 1, :, None].to_broadcast([P, 2, UB, E]), ALU.mult).then_inc(s_gread, 1)
                yield
                dve.wait_ge(s_gread, pair + 1)
                dve.tensor_tensor(g1[:, :, :], gx[:, :, :], bgb[:, None, :].to_broadcast([P, PB, E]), ALU.add)\
                    .then_inc(s_top, 1)
                yield
                after(1)
                dve.tensor_reduce(m1[:, :], g1[:, :, :], AX.X, ALU.max).then_inc(s_top, 1)
                yield
                after(2)
                dve.tensor_tensor(eq[:, :, :], g1[:, :, :], per_graph(m1), ALU.is_equal).then_inc(s_top, 1)
                yield
                after(3)
                dve.tensor_tensor(eqw[:, :, :], eq[:, :, :], w_bc, ALU.mult).then_inc(s_top, 1)
                yield
                after(4)
                dve.tensor_reduce(w1[:, :], eqw[:, :, :], AX.X, ALU.max).then_inc(s_top, 1)
                yield
                after(5)
                dve.tensor_tensor(eq[:, :, :], w_bc, per_graph(w1), ALU.is_equal).then_inc(s_top, 1)
                yield
                after(6)
                dve.scalar_tensor_tensor(g2[:, :, :], eq[:, :, :], -BIG, g1[:, :, :], ALU.mult, ALU.add)\
                    .then_inc(s_top, 1)
                yield
                after(7)
                dve.tensor_reduce(m2[:, :], g2[:, :, :], AX.X, ALU.max).then_inc(s_top, 1)
                yield
                after(8)
                dve.tensor_tensor(eq[:, :, :], g2[:, :, :], per_graph(m2), ALU.is_equal).then_inc(s_top, 1)
                yield
                after(9)
                dve.tensor_tensor(eqw[:, :, :], eq[:, :, :], w_bc, ALU.mult).then_inc(s_top, 1)
                yield
                after(10)
                dve.tensor_reduce(w2[:, :], eqw[:, :, :], AX.X, ALU.max).then_inc(s_top, 1)
                yield
                after(11)
                dve.tensor_tensor(wx[:, :], w1[:, :], w2[:, :], ALU.max)
                dve.tensor_tensor(wn[:, :], w1[:, :], w2[:, :], ALU.min).then_inc(s_top, 1)
                yield
                after(12)
                dve.scalar_tensor_tensor(code[:, :], wx[:, :], float(E), wn[:, :], ALU.mult, ALU.add)\
                    .then_inc(s_top, 1)
                yield
                after(13)
                if not isinstance(pair, int) or pair > 0:
                    dve.wait_ge(s_cnt, pair)
                dve.tensor_tensor(onehot[:, :, :], tab[:, None, T_CODE:T_CODE + NG].to_broadcast([P, PB, NG]),
                                  code[:, :, None].to_broadcast([P, PB, NG]), ALU.is_equal).then_inc(s_hot, 1)
                yield

            def ranks_of_own(pair):
                dve.wait_ge(s_rank, pair + 1)
                dve.tensor_tensor(rank_m[:, :, :], ps_r, onehot[:, :, :], ALU.mult).then_inc(s_rread, 1)

            def positions(pair, buf):
                dve.wait_ge(s_rread, pair + 1)
                with nc.allow_low_precision(reason="whole numbers below 2^24, summed in float32"):
                    dve.tensor_reduce(pos[:, buf], rank_m[:, :, :], AX.X, ALU.add).then_inc(s_pos, 1)

            def slots(k):
                for q in range(A_DEEP):
                    n = A_DEEP * k + q
                    choosing = q % 2 == 0 and unit(k, q, 4)
                    placing = q % 2 == 1 and unit(k, q, 5)
                    pair = A_DEEP // 2 * k + q // 2 - 2
                    choice = top2(pair) if choosing else iter(())
                    if unit(k, q, 2):
                        x1(*back(k, q, 2, A_DEEP))
                    if slot(k, q, 1):
                        rstds(*back(k, q, 1, A_DEEP))
                    if placing:
                        ranks_of_own(pair)
                    if slot(k, q):
                        for b in range(UB):
                            if unit(k, q):
                                last = stats1(k, q, b)
                            if b == 0 and unit(k, q, 1):
                                coefs(*back(k, q, 1, A_DEEP))
                            if b > 0:
                                next(choice, None)
                    if placing:
                        positions(pair, (q // 2 - 2) % 4)
                    for b in range(UB):
                        if unit(k, q, 1):
                            product(*back(k, q, 1, A_DEEP), b)
                        next(choice, None)
                    if slot(k, q):
                        for b in range(UB):
                            if unit(k, q, 2):
                                last = stats2(k, q, b)
                            if b % 2:
                                next(choice, None)
                        last.then_inc(s_bn, 1)
                        dve.wait_ge(s_bn, 2 * n + 1)
                        if unit(k, q, 4):
                            dve.wait_ge(s_meta, n - 3)
                        dve.sem_inc(s_turn_dve, 1)
                        for w in range(2):
                            for b in range(UB):
                                if unit(k, q, 2 * w):
                                    last = aggregate(k, q, w, b)
                                if b % 2:
                                    next(choice, None)
                        last.then_inc(s_bn, 1)
                        next(choice, None)
                        variances(k, q)
                    for _ in choice:
                        pass

            dve.wait_ge(s_exp, 16 * (3 + 2 * HT))
            g = 0
            for a in range(E - 1):
                n = E - 1 - a
                last = dve.tensor_tensor(b2_pair[:, g:g + n], b2b[:, a:a + 1].to_broadcast([P, n, P]),
                                         b2b[:, a + 1:E], ALU.add)
                g += n
            last.then_inc(s_b2, 1)
            slots(0)
            with dve.Fori(1, A_LOOPS) as k:
                slots(k)
            slots(A_LOOPS)

            STEPS = 0

            def step(ins):
                nonlocal STEPS
                STEPS += 1
                ins.then_inc(s_tb, 1)
                dve.wait_ge(s_tb, STEPS)

            base = tab[:, T_BASE:T_BASE + NG]
            chunk_no = tab[:, T_CHUNK:T_CHUNK + 1]
            vals = tab[:, T_VALS:T_VALS + 4 * NG].rearrange("p (v g) -> p v g", v=4)
            dve.wait_ge(s_cnt, UNITS // 2)
            step(dve.tensor_tensor(cnt[:, :], ps_r[:, 0], base, ALU.subtract))
            step(dve.tensor_scalar(cnt_up[:, :], cnt[:, :], float(C - 1), None, ALU.add))
            step(dve.tensor_scalar(nch_i[:, :], cnt_up[:, :], C.bit_length() - 1, None, ALU.logical_shift_right))
            step(dve.tensor_copy(nch[:, :], nch_i[:, :]))
            step(dve.tensor_tensor_scan(c_end[:, :], nch[:, :], zero_g[:, :], 0.0, ALU.add, ALU.add))
            step(dve.tensor_tensor(c_beg[:, :], c_end[:, :], nch[:, :], ALU.subtract))
            dve.tensor_scalar(in_beg[:, :], c_beg[:, :], chunk_no, None, ALU.is_le)
            dve.tensor_scalar(in_end[:, :], c_end[:, :], chunk_no, None, ALU.is_gt)
            dve.tensor_scalar(at[:, :], c_beg[:, :], chunk_no, -float(C), ALU.subtract, ALU.mult)
            step(dve.tensor_scalar(last_at[:, :], cnt[:, :], -float(C), None, ALU.add))
            dve.tensor_tensor(in_g[:, :], in_beg[:, :], in_end[:, :], ALU.mult)
            step(dve.tensor_tensor(near[:, :], at[:, :], last_at[:, :], ALU.min))
            step(dve.tensor_tensor(vals[:, 0], near[:, :], base, ALU.add))
            step(dve.tensor_tensor(picked[:, :, :], vals, in_g[:, None, :].to_broadcast([P, 4, NG]), ALU.mult))
            with nc.allow_low_precision(reason="whole numbers below 2^24, summed in float32"):
                dve.tensor_reduce(chunk_cols[:, :], picked[:, :, :], AX.X, ALU.add).then_inc(s_tbd, 1)
            dve.wait_ge(s_tbm, 16)

            def value(n, v, top):
                return dve.value_load(chunk_tab[0:1, bass.ds(4 * n + v, 1)], min_val=0, max_val=top)

            def prepare(k, q):
                n, t = DEEP * k + q, q % 2
                if chunk(k, q, DEEP):
                    dve.wait_ge(s_y, n + 1 - DEEP)
                for s in range(2):
                    e = value(n, 1 + s, E - 1)
                    last = dve.tensor_copy(wbuf[:, q, s], experts[:, bass.ds(e, 1)].rearrange("p o c -> p (o c)"))
                last.then_inc(s_w, 1)
                dve.wait_ge(s_rows[q], 16 * k + 16)
                if chunk(k, q, 2):
                    dve.wait_ge(s_psxs, n - 1)
                for j in range(CJ):
                    last = dve.tensor_scalar(xs[:, t, j], rows[:, q, j, 0:P], rows[:, q, j, MEAN:MEAN + 1],
                                             rows[:, q, j, RSTD:RSTD + 1], ALU.subtract, ALU.mult)
                last.then_inc(s_xs, 1)
                g = value(n, 3, NG - 1)
                if chunk(k, q, DEEP):
                    dve.wait_ge(s_out[q], 16 * CJ * k)
                dve.tensor_copy(out_ids[:, q], rows_u[:, q, :, ID])
                dve.tensor_tensor(xb[:, q], rows[:, q, :, 0:P],
                                  b2_pair[:, bass.ds(g, 1)].to_broadcast([P, CJ, P]), ALU.add).then_inc(s_xb, 1)

            def finish(k, q):
                n, t = DEEP * k + q, q % 2
                dve.wait_ge(s_y, n + 1)
                if chunk(k, q, DEEP):
                    dve.wait_ge(s_out[q], 16 * CJ * k)
                dve.wait_ge(s_xb, n + 1)
                dve.tensor_tensor(ob[:, q], ps_y[t], xb[:, q], ALU.add).then_inc(s_ob, 1)

            def chunk_slots(k):
                for q in range(DEEP):
                    if chunk(k, q):
                        prepare(k, q)
                    if chunk(k, q, 3):
                        finish(*back(k, q, 3, DEEP))

            chunk_slots(0)
            with dve.Fori(1, CQUADS) as k:
                chunk_slots(k)
            chunk_slots(CQUADS)

        @block.tensor
        def _(pe):
            def transposes(k, q):
                n, m = A_DEEP * k + q, q % LOADS
                pe.wait_ge(s_adj[m], 16 * (A_DEEP // LOADS * k + q // LOADS + 1))
                if unit(k, q, 1):
                    pe.wait_ge(s_aT, n)
                for b in range(UB):
                    last = pe.transpose(ps_a[:, b], ain[:, m, b], ident)
                last.then_inc(s_psa, 1)
                pe.wait_ge(s_x[m], 16 * (A_DEEP // LOADS * k + q // LOADS + 1))
                if unit(k, q, 1):
                    pe.wait_ge(s_xT, n)
                for b in range(UB):
                    last = pe.transpose(ps_x[:, b], xin[:, m, b], ident)
                last.then_inc(s_psxT, 1)

            def products(k, q):
                n, t = A_DEEP * k + q, q % 2
                pe.wait_ge(s_xT, n + 1)
                if unit(k, q, 1):
                    pe.wait_ge(s_pr, n)
                for b in range(UB):
                    last = pe.matmul(ps_pr[b // 2][:, b % 2], xT[:, t, b], w_cen[:, :, :], start=True, stop=True)
                last.then_inc(s_pspr, 1)

            def conv(k, q):
                n, t = A_DEEP * k + q, q % 2
                pe.wait_ge(s_pr, n + 1)
                if unit(k, q, 1):
                    pe.wait_ge(s_x1, n)
                pe.matmul(ps_c, ident, pr[:, t, :, 1], start=True, stop=False, skip_group_check=True)
                pe.wait_ge(s_aT, n + 1)
                for b in range(UB):
                    last = pe.matmul(ps_c[:, b], aT[:, t, b], pr[:, t, b, 0], start=False, stop=b == UB - 1,
                                     skip_group_check=True)
                last.then_inc(s_conv, 1)

            def x1_transposes(k, q):
                n = A_DEEP * k + q
                pe.wait_ge(s_x1, n + 1)
                if unit(k, q, 1):
                    pe.wait_ge(s_x1T, n)
                for b in range(UB):
                    last = pe.transpose(ps_x1[:, b], row[:, q, b, 0:P], ident)
                last.then_inc(s_psx1, 1)

            def gates(k, q):
                n, t = A_DEEP * k + q, q % 2
                pe.wait_ge(s_x1T, n + 1)
                if t == 0 and unit(k, q, 1):
                    pe.wait_ge(s_gread, A_DEEP // 2 * k + q // 2)
                for b in range(UB):
                    last = pe.matmul(ps_g[:, UB * t + b], x1T[:, t, b], wg[:, :], start=True, stop=True)
                last.then_inc(s_gate, 1)

            def ranks(pair):
                pe.wait_ge(s_hot, pair + 1)
                last = pe.matmul(ps_r, tri[:, :], onehot[:, :, :], start=False, stop=False, skip_group_check=True)
                for b in range(PB - 1):
                    m = PB - 1 - b
                    last = pe.matmul(ps_r[:, b + 1:PB], ones[:, :], onehot[:, b:b + 1].to_broadcast([P, m, NG]),
                                     start=False, stop=False, skip_group_check=True)
                last.then_inc(s_rank, 1)

            def counts(pair):
                pe.wait_ge(s_rread, pair + 1)
                pe.matmul(ps_r, tri_rest[:, :], onehot[:, :, :], start=False, stop=False, skip_group_check=True)
                for b in range(1, PB):
                    last = pe.matmul(ps_r[:, 0:b], ones[:, :], onehot[:, b:b + 1].to_broadcast([P, b, NG]),
                                     start=False, stop=False, skip_group_check=True)
                last.then_inc(s_cnt, 1)

            def slots(k):
                for q in range(A_DEEP):
                    pair = A_DEEP // 2 * k + q // 2
                    if unit(k, q):
                        transposes(k, q)
                    if q % 2 == 1 and unit(k, q, 5):
                        ranks(pair - 2)
                    if unit(k, q, 2):
                        x1_transposes(*back(k, q, 2, A_DEEP))
                    if unit(k, q, 1):
                        conv(*back(k, q, 1, A_DEEP))
                    if unit(k, q):
                        products(k, q)
                    if unit(k, q, 2):
                        gates(*back(k, q, 2, A_DEEP))
                    if q % 2 == 0 and unit(k, q, 6):
                        counts(pair - 3)

            pe.wait_ge(s_tab, 16)
            pe.wait_ge(s_ready, 5)
            pe.wait_ge(s_setup, 6)
            pe.matmul(ps_w, center[:, :], w_gam[:, :, :], start=True, stop=True)
            pe.matmul(ps_cb, bet_mat[:, :], w_in[:, :, :], start=True, stop=True)
            pe.wait_ge(s_small, 16 * SMALL)
            pe.matmul(ps_wg, center[:, :], wg_in[:, :], start=True, stop=True).then_inc(s_fold, 1)
            pe.wait_ge(s_setup, 10)
            pe.matmul(ps_r, ones_row[:, :], base_row[:, :, :], start=True, stop=False, skip_group_check=True)
            slots(0)
            with pe.Fori(1, A_LOOPS) as k:
                slots(k)
            slots(A_LOOPS)

            def chunk_transpose(k, q):
                n, t = DEEP * k + q, q % 2
                pe.wait_ge(s_xs, n + 1)
                if chunk(k, q, 2):
                    pe.wait_ge(s_xsT, n - 1)
                for j in range(CJ):
                    last = pe.transpose(ps_xs[t][:, j * P:(j + 1) * P], xs[:, t, j], ident)
                last.then_inc(s_psxs, 1)

            def up(k, q):
                n, t = DEEP * k + q, q % 2
                pe.wait_ge(s_w, n + 1)
                pe.wait_ge(s_xsT, n + 1)
                if chunk(k, q, 2):
                    pe.wait_ge(s_gel, n - 1)
                for s in range(2):
                    for h in range(HT):
                        last = pe.matmul(ps_h[t][s][:, h], wbuf[:, q, s, h * P:(h + 1) * P], xsT[:, t],
                                         start=True, stop=True)
                last.then_inc(s_h, 1)

            def down(k, q):
                n, t = DEEP * k + q, q % 2
                pe.wait_ge(s_gel, n + 1)
                if chunk(k, q, 2):
                    pe.wait_ge(s_ob, n - 1)
                for j in range(CJ):
                    for s in range(2):
                        for h in range(HT):
                            last = pe.matmul(ps_y[t][:, j], gT[:, t, s, h, j * P:(j + 1) * P],
                                             wbuf[:, q, s, HID + h * P:HID + (h + 1) * P],
                                             start=s + h == 0, stop=s + h == HT)
                last.then_inc(s_y, 1)

            def chunk_slots(k):
                for q in range(DEEP):
                    if chunk(k, q):
                        chunk_transpose(k, q)
                    if chunk(k, q, 1):
                        up(*back(k, q, 1, DEEP))
                    if chunk(k, q, 2):
                        down(*back(k, q, 2, DEEP))

            chunk_slots(0)
            with pe.Fori(1, CQUADS) as k:
                chunk_slots(k)
            chunk_slots(CQUADS)


INPUTS = ["x", "adj", "L0_gnn_W_rel", "L0_gnn_b_rel", "L0_gnn_W_root", "L0_gnn_ln_gamma", "L0_gnn_ln_beta",
          "L0_ffn_Wg", "L0_ffn_bg", "L0_ffn_W1", "L0_ffn_b1", "L0_ffn_W2", "L0_ffn_b2"]


def kernel(**inputs):
    import numpy as _np
    import concourse.bacc as _bacc
    from concourse import mybir as _mybir
    from concourse.bass_utils import run_bass_kernel_spmd as _run

    nc = _bacc.Bacc("TRN2", target_bir_lowering=False, num_devices=1)
    arrays, args = {}, []
    named = [(n, _np.ascontiguousarray(inputs[n])) for n in INPUTS]
    named += list(zip(["shape_table", "token_ids", "padding_rows"], constants()))
    for name, a in named:
        arrays[f"in_{name}"] = a
        args.append(nc.dram_tensor(f"in_{name}", a.shape, _mybir.dt.from_np(a.dtype), kind="ExternalInput").ap())
    out = nc.dram_tensor("out_rows", (TOKENS, P), _mybir.dt.float32, kind="ExternalOutput").ap()
    build(nc, *args, out)
    r = _run(nc, [arrays], core_ids=[0])
    return r.results[0]["out_rows"].reshape(GRAPHS, P, P)
```

```python
from contextlib import ExitStack

import numpy as np

import concourse.bass as bass
from concourse import mybir

F32 = mybir.dt.float32
F32R = mybir.dt.float32r
BF16 = mybir.dt.bfloat16
U32 = mybir.dt.uint32
I32 = mybir.dt.int32
ALU = mybir.AluOpType
ACT = mybir.ActivationFunctionType
AX = mybir.AxisListType

P = 128
GRAPHS = 128
TOKENS = GRAPHS * P
UB = 4
UNITS = GRAPHS // UB
A_DEEP = 8
A_LOOPS = UNITS // A_DEEP
LOADS = 4
E = 8
HID = 256
HT = HID // P
EPS = 1e-5
PAIRS = [(a, b) for a in range(E) for b in range(a + 1, E)]
NG = len(PAIRS)
CJ = 2
C = CJ * P
REGION = C + TOKENS
HALVES = (TOKENS - NG) // P + NG
NARROW = NG + 1
WIDE = (HALVES - NARROW + 1) // 2
CHUNKS = WIDE + NARROW
BUFS = 4
C_DEEP = 3 * BUFS
LEFT_OUT = {CJ: HID, 1: 0}
C_LOOPS = NARROW // BUFS
LATE = C_DEEP * (C_LOOPS + 1) - CHUNKS
ROW = 132
ID, MEAN, VAR, RSTD = P, P + 1, P + 2, P + 3
PACK = HID + HT * P + HT
BIG = 1e38

T_IDENT = 0
T_TRI = T_IDENT + P
T_W = T_TRI + P
T_CODE = T_W + E
T_BASE = T_CODE + NG
T_VALS = T_BASE + NG
T_PAIR = T_VALS + 5 * NG
T_SINGLE = T_PAIR + 1
T_SIZE = T_SINGLE + 1
T_ROW = T_SIZE + 1
T_COLS = T_ROW + CJ + 1


def tiles(k, q):
    return 1 if q % 3 == 1 and (not isinstance(k, int) or k > 0 or q >= C_DEEP - BUFS) else CJ


NARROW_CHUNKS = slice(C_DEEP - 2 - LATE, CHUNKS, 3)


def constants():
    t = np.zeros((P, T_COLS), np.float32)
    t[:, T_IDENT:T_IDENT + P] = np.eye(P)
    t[:, T_TRI:T_TRI + P] = np.triu(np.ones((P, P)), 1)
    t[:, T_W:T_W + E] = weight = 2 ** np.arange(E)[::-1]
    t[:, T_CODE:T_CODE + NG] = [weight[a] + weight[b] for a, b in PAIRS]
    t[:, T_BASE:T_BASE + NG] = [g * REGION + C for g in range(NG)]
    t[:, T_VALS + NG:T_VALS + 2 * NG] = [a for a, b in PAIRS]
    t[:, T_VALS + 2 * NG:T_VALS + 3 * NG] = [b for a, b in PAIRS]
    t[:, T_VALS + 3 * NG:T_VALS + 4 * NG] = np.arange(NG)
    narrow = np.zeros(P, bool)
    narrow[NARROW_CHUNKS] = True
    assert narrow.sum() == NARROW == C_DEEP // 3 * C_LOOPS + 1 and 2 * WIDE + NARROW >= HALVES
    t[:, T_PAIR] = np.where(narrow, -1, np.cumsum(~narrow) - 1)
    t[:, T_SINGLE] = np.where(narrow, np.cumsum(narrow) - 1, -1)
    t[CHUNKS:, T_PAIR] = -1
    t[:, T_SIZE] = np.where(narrow, P, C)
    t[:, T_ROW:T_ROW + CJ] = CJ * np.arange(P)[:, None] + np.arange(CJ)
    t[:, T_ROW + CJ] = np.arange(P)
    ids = (np.arange(P)[:, None] + P * np.arange(GRAPHS)[None, :]).astype(np.uint32)
    pad = np.zeros((P, CJ * ROW), np.uint32)
    pad[:, ID::ROW] = TOKENS
    return t, ids, pad


def back(k, q, d, deep):
    return (k, q - d) if q >= d else (k - 1, q - d + deep)


def exists(k, q, d, deep, n):
    return not isinstance(k, int) or 0 <= deep * k + q - d < n


def unit(k, q, d=0):
    return exists(k, q, d, A_DEEP, UNITS)


def number(k, q):
    return C_DEEP * k + q - LATE


def chunk(k, q, d=0):
    return exists(k, q, LATE + d, C_DEEP, CHUNKS)


def wide_chunks(k, q):
    if isinstance(k, int) and k == 0:
        return sum(tiles(0, i) == CJ for i in range(LATE, q + 1))
    body = sum(tiles(1, i) == CJ for i in range(C_DEEP))
    return wide_chunks(0, C_DEEP - 1) + body * (k - 1) + sum(tiles(1, i) == CJ for i in range(q + 1))


def scattered(k, q):
    if isinstance(k, int) and k == 0:
        return 16 * sum(tiles(0, i) for i in range(LATE + q % BUFS, q, BUFS))
    first = sum(tiles(0, i) for i in range(LATE + q % BUFS, C_DEEP, BUFS))
    body = sum(tiles(1, i) for i in range(0, C_DEEP, BUFS))
    return 16 * (first + body * (k - 1) + sum(tiles(1, i) for i in range(q % BUFS, q, BUFS)))


def build(nc, x, adj, W_rel, b_rel, W_root, gamma, beta, Wg, bg, W1, b1, W2, b2, table, ids, pad, out):
    rows_dram = nc.dram_tensor("rows_by_group", [NG * REGION, ROW], F32, kind="Internal").ap()

    with ExitStack() as ctx:
        def sb(name, shape, dt=F32):
            return ctx.enter_context(nc.sbuf_tensor(name, shape, dt))

        def sem(name):
            return ctx.enter_context(nc.semaphore(name))

        def sems(name, n):
            return [sem(f"{name}{i}") for i in range(n)]

        tab = sb("tab", [P, T_COLS])
        ident = tab[:, T_IDENT:T_IDENT + P]
        tok_ids = sb("tok_ids", [P, GRAPHS], U32)
        pad_rows = sb("pad_rows", [P, CJ * ROW], U32)
        tri = sb("tri", [P, P], BF16)
        tri_rest = sb("tri_rest", [P, P], BF16)
        ones = sb("ones", [P, P], BF16)
        ones_f = sb("ones_f", [P, P])
        ones_row = sb("ones_row", [1, P])
        base_row = sb("base_row", [1, 2 * UB, NG])
        w_in = sb("w_in", [P, 2, P])
        w_gam = sb("w_gam", [P, 2, P])
        center = sb("center", [P, P])
        gam = sb("gam", [P, 1])
        bet = sb("bet", [P, 1])
        bet_mat = sb("bet_mat", [P, P])
        brel_b = sb("brel_b", [P, P])
        const_b = sb("const_b", [P, 2, P])
        part = sb("part", [P, 2, P])
        const_hml = sb("const_hml", [P, 3, 2, P], BF16)
        const_k = sb("const_k", [P, 2, P], BF16)
        wg_in = sb("wg_in", [P, E])
        wg = sb("wg", [P, E])
        bgb = sb("bgb", [P, E])
        w1_hl = sb("w1_hl", [P, E, 2, HID], F32R)
        experts = sb("experts", [P, E, PACK])
        b2b = sb("b2b", [P, E, P])
        b2_pair = sb("b2_pair", [P, NG, P])

        xin = sb("xin", [P, LOADS, UB, P])
        ain = sb("ain", [P, LOADS, UB, P])
        st1 = sb("st1", [P, 2, UB, 6])
        mv1 = sb("mv1", [P, 2, UB, 2])
        var1 = sb("var1", [P, 2, 2, UB])
        std1 = sb("std1", [P, 2, 2, UB])
        rstd1 = sb("rstd1", [P, 4, 2, UB])
        xr_scale = sb("xr_scale", [P, 4, UB])
        bias = sb("bias", [P, 4, 2, UB])
        st2 = sb("st2", [P, 2, UB, 6])
        var2 = sb("var2", [P, 2, UB])
        std2 = sb("std2", [P, 2, UB])
        z = sb("z", [P, 2, UB, P])
        zT = sb("zT", [P, 2, UB, P])
        aT = sb("aT", [P, 2, UB, P])
        pr = sb("pr", [P, 2, UB, P])
        xr = sb("xr", [P, 2, UB, P])
        row = sb("row", [P, A_DEEP, UB, ROW])
        row_u = row[:, :, :, :].bitcast(U32)
        x1T = sb("x1T", [P, 2, UB, P])
        PB = 2 * UB
        gx = sb("gx", [P, PB, E])
        g1 = sb("g1", [P, PB, E])
        g2 = sb("g2", [P, PB, E])
        eq = sb("eq", [P, PB, E])
        eqw = sb("eqw", [P, PB, E])
        m1 = sb("m1", [P, PB])
        m2 = sb("m2", [P, PB])
        w1 = sb("w1", [P, PB])
        w2 = sb("w2", [P, PB])
        code = sb("code", [P, PB])
        onehot = sb("onehot", [P, PB, NG], BF16)
        rank_m = sb("rank_m", [P, PB, NG])
        pos = sb("pos", [P, 4, PB], U32)

        cnt = sb("cnt", [P, NG])
        cnt_up = sb("cnt_up", [P, NG], I32)
        halves_i = sb("halves_i", [P, 2, NG], I32)
        halves = sb("halves", [P, 2, NG])
        over = sb("over", [P, 1])
        is_over = sb("is_over", [P, 1])
        over_i = sb("over_i", [P, 1], I32)
        over_parts_i = sb("over_parts_i", [P, 2], I32)
        over_parts = sb("over_parts", [P, 2])
        pair_no = sb("pair_no", [P, 1])
        pair_at = sb("pair_at", [P, 1])
        gelu_warm = sb("gelu_warm", [P, 1])
        zero_g = sb("zero_g", [P, NG])
        c_end = sb("c_end", [P, 2, NG])
        c_beg = sb("c_beg", [P, 2, NG])
        in_beg = sb("in_beg", [P, 2, NG])
        in_end = sb("in_end", [P, 2, NG])
        in_g = sb("in_g", [P, NG])
        at_both = sb("at_both", [P, 2, NG])
        in_both = sb("in_both", [P, 2, NG])
        at = sb("at", [P, NG])
        last_at = sb("last_at", [P, NG])
        near = sb("near", [P, NG])
        picked = sb("picked", [P, 5, NG])
        chunk_cols = sb("chunk_cols", [P, 5], I32)
        repeated = sb("repeated", [P, P])
        drop = sb("drop", [P, P, CJ])
        chunk_tab = sb("chunk_tab", [1, CHUNKS * 4], I32)

        rows = sb("rows", [P, BUFS, CJ, ROW])
        rows_u = rows[:, :, :, :].bitcast(U32)
        row_ids = sb("row_ids", [P, BUFS, CJ], U32)
        out_ids = sb("out_ids", [P, BUFS, CJ], U32)
        w1buf = sb("w1buf", [P, BUFS, 2, 2, HID], F32R)
        wbuf = sb("wbuf", [P, BUFS, 2, PACK])
        xs = sb("xs", [P, 2, CJ, P])
        xsT = sb("xsT", [P, 2, 2, C], F32R)
        xsT_narrow = sb("xsT_narrow", [P, P])
        xb = sb("xb", [P, BUFS, CJ, P])
        gT = sb("gT", [P, 2, 2, HT, C])
        ob = sb("ob", [P, BUFS, CJ, P])

        bank = [ctx.enter_context(nc.psum_tensor(f"bank{i}", [P, 512], F32)) for i in range(8)]

        def four(b):
            return b[:, :].rearrange("p (b c) -> p b c", b=UB)

        ps_a, ps_z, ps_x1, ps_p = four(bank[0]), four(bank[1]), four(bank[3]), four(bank[4])
        ps_c = [four(bank[2]), four(bank[5])]
        ps_g = bank[6][:, 0:PB * E].rearrange("p (b e) -> p b e", b=PB)
        ps_r = bank[7][:, 0:PB * NG].rearrange("p (b g) -> p b g", b=PB)
        ps_cb = bank[5][:, 0:2 * P].rearrange("p (w c) -> p w c", w=2)
        ps_wg = bank[6][:, 0:E]
        ps_xs = [bank[0][:, 0:C], bank[7][:, 0:C]]
        ps_h = [[bank[1 + 2 * t + s][:, :].rearrange("p (k c) -> p k c", k=HT) for s in range(2)] for t in range(2)]
        ps_y = [bank[5 + t][:, 0:C].rearrange("p (j c) -> p j c", j=CJ) for t in range(2)]

        s_tab = sem("tables_in")
        s_small = sem("small_weights_in")
        s_exp = sem("experts_in")
        s_pad = sem("padding_rows_out")
        s_ready = sem("constants_built")
        s_setup = sem("setup_step")
        s_fold = sem("folded_weights_in_psum")
        s_const = sem("constants_step")
        s_ids_in = sem("token_ids_and_padding_rows_in")
        s_b2 = sem("b2_pairs_and_w1_parts_step")
        s_x = sems("x_in", LOADS)
        s_adj = sems("adj_in", LOADS)
        s_psa = sem("adjT_in_psum")
        s_aT = sem("adjT_ready")
        s_z = sem("z_ready")
        s_psz = sem("zT_in_psum")
        s_zT = sem("zT_ready")
        s_pspr = sem("products_in_psum")
        s_pr = sem("h_wrel_ready")
        s_conv = sem("conv_in_psum")
        s_bn1 = sem("ln1_statistics_step")
        s_var1 = sem("ln1_variances_ready")
        s_std1 = sem("ln1_stds_ready")
        s_rstd1 = sem("ln1_rstds_ready")
        s_bn2 = sem("ln2_statistics_step")
        s_var2 = sem("ln2_variances_ready")
        s_std2 = sem("ln2_stds_ready")
        s_rstd2 = sem("ln2_rstds_ready")
        s_coef = sem("coefs_ready")
        s_xr = sem("residual_ready")
        s_xr_last = sem("residual_of_last_graph_ready")
        s_x1 = sem("x1_ready")
        s_psx1 = sem("x1T_in_psum")
        s_x1T = sem("x1T_ready")
        s_gate = sem("gates_in_psum")
        s_top = sem("top2_step")
        s_gread = sem("gates_read")
        s_hot = sem("onehot_ready")
        s_rank = sem("ranks_in_psum")
        s_rread = sem("ranks_read")
        s_cnt = sem("counts_in_psum")
        s_pos = sem("positions_ready")
        s_rid = sem("row_ids_ready")
        s_scat = sems("rows_scattered", A_DEEP)
        s_tb = sem("chunk_table_step")
        s_tbd = sem("chunk_table_ready")
        s_rep = sem("repeated_rows_step")
        s_repb = sem("repeated_rows_in_psum")
        s_tbm = sem("chunk_table_in_row")
        s_rows = sems("rows_in", BUFS)
        s_w = sem("weights_copied")
        s_xs = sem("chunk_normed")
        s_xb = sem("rows_used")
        s_ids = sem("ids_taken")
        s_w2 = sem("second_weights_copied")
        s_psxs = sem("chunk_xT_in_psum")
        s_xsT = sem("chunk_xT_high_part_ready")
        s_xsL = sem("chunk_xT_low_part_ready")
        s_h = sem("hidden_in_psum")
        s_gel = sem("gelu_ready")
        s_y = sem("y_in_psum")
        s_ob = sem("out_rows_ready")
        s_out = sems("out_rows_scattered", BUFS)

        s_turn_pool = sem("pool_wait_done")
        s_turn_dve = sem("dve_wait_done")

        SMALL = 7
        EXPERT_LOADS = 2 + 2 * HT
        block = ctx.enter_context(nc.Block())

        @block.sync
        def _(sp):
            sp.dma_start(tab[:, :], table).then_inc(s_tab, 16)

            def load(k, q):
                m, n = q % LOADS, A_DEEP * k + q
                if unit(k, q, LOADS):
                    sp.wait_ge(s_xr, n + 1 - LOADS)
                    sp.wait_ge(s_xr_last, n + 1 - LOADS)
                    sp.wait_ge(s_psa, n + 1 - LOADS)
                sp.dma_start(xin[:, m], x[bass.ds(UB * A_DEEP * k + UB * q, UB)].rearrange("b p c -> p b c"))\
                    .then_inc(s_x[m], 16)
                sp.dma_start(ain[:, m], adj[bass.ds(UB * A_DEEP * k + UB * q, UB)].rearrange("b p c -> p b c"))\
                    .then_inc(s_adj[m], 16)

            for q in range(LOADS):
                load(0, q)
            sp.dma_start(b2b[:, :, :], b2[None, :, :].to_broadcast([P, E, P])).then_inc(s_exp, 16)
            sp.dma_start(experts[:, :, 0:HID], W1.rearrange("e d h -> d e h")).then_inc(s_exp, 16)
            for k in range(HT):
                sp.dma_start(experts[:, :, HID + k * P:HID + (k + 1) * P],
                             W2[:, k * P:(k + 1) * P, :].rearrange("e h d -> h e d")).then_inc(s_exp, 16)
                sp.dma_start(experts[:, :, HID + HT * P + k], b1[:, k * P:(k + 1) * P].rearrange("e h -> h e"),
                             allow_slow_non_contiguous=True).then_inc(s_exp, 16)
            sp.dma_start(pad_rows[:, :], pad).then_inc(s_ids_in, 16)
            sp.dma_start(tok_ids[:, :], ids).then_inc(s_ids_in, 16)
            sp.wait_ge(s_ids_in, 32)
            padding = rows_dram.bitcast(U32).rearrange("(g r) c -> g r c", g=NG)[:, 0:C, :]\
                .rearrange("g (p j) c -> p g (j c)", j=CJ)
            some = NG // (A_DEEP - LOADS)
            for q in range(LOADS, A_DEEP):
                load(0, q)
                g = some * (q - LOADS)
                sp.dma_start(padding[:, g:g + some], pad_rows[:, None, :].to_broadcast([P, some, CJ * ROW]))\
                    .then_inc(s_pad, 16)
            with sp.Fori(1, A_LOOPS) as k:
                for q in range(A_DEEP):
                    load(k, q)

            sp.wait_ge(s_tbd, 1)
            sp.dma_start(chunk_tab[0:1, :].rearrange("o (c v) -> o c v", v=4), chunk_cols[0:CHUNKS, 0:4])\
                .then_inc(s_tbm, 16)
            sp.wait_ge(s_tbm, 16)
            sp.wait_ge(s_pad, 16 * (A_DEEP - LOADS))
            for q in range(A_DEEP):
                sp.wait_ge(s_scat[q], 16 * UB * A_LOOPS)

            def load_rows(k, q):
                n, m, size = number(k, q), q % BUFS, tiles(k, q) * P
                if chunk(k, q, BUFS):
                    sp.wait_ge(s_xb, n + 1 - BUFS)
                first = sp.value_load(chunk_tab[0:1, bass.ds(4 * n, 1)], min_val=0, max_val=NG * REGION - size)
                sp.dma_start(rows[:, m, 0:tiles(k, q)],
                             rows_dram[bass.ds(first, size)].rearrange("(p j) c -> p j c", j=tiles(k, q)))\
                    .then_inc(s_rows[m], 16)

            for q in range(LATE, C_DEEP):
                load_rows(0, q)
            with sp.Fori(1, C_LOOPS + 1) as k:
                for q in range(C_DEEP):
                    load_rows(k, q)
            for m in range(BUFS):
                sp.wait_ge(s_out[m], scattered(C_LOOPS + 1, m))

        @block.gpsimd
        def _(pool):
            pool.memset(ones[:, :], 1.0).then_inc(s_ready, 1)
            pool.memset(ones_row[:, :], 1.0).then_inc(s_ready, 1)
            pool.memset(ones_f[:, :], 1.0).then_inc(s_ready, 1)
            pool.memset(zero_g[:, :], 0.0).then_inc(s_ready, 1)
            pool.wait_ge(s_exp, 16 * EXPERT_LOADS)
            g = 0
            for a in range(E - 1):
                n = E - 1 - a
                pool.tensor_tensor(b2_pair[:, g:g + n], b2b[:, a:a + 1].to_broadcast([P, n, P]), b2b[:, a + 1:E],
                                   ALU.add)
                g += n
            pool.tensor_copy(w1_hl[:, :, 0], experts[:, :, 0:HID]).then_inc(s_b2, 1)
            pool.wait_ge(s_b2, 1)
            pool.tensor_tensor(w1_hl[:, :, 1], experts[:, :, 0:HID], w1_hl[:, :, 0].bitcast(F32), ALU.subtract)\
                .then_inc(s_b2, 1)
            pool.wait_ge(s_ids_in, 32)

            def scatter(k, q):
                n, pair = A_DEEP * k + q, A_DEEP // 2 * k + q // 2
                if unit(k, q, A_DEEP):
                    pool.wait_ge(s_scat[q], 16 * UB * k)
                pool.sem_inc(s_turn_pool, 1)
                pool.tensor_copy(row_u[:, q, :, ID], tok_ids[:, bass.ds(UB * A_DEEP * k + UB * q, UB)])\
                    .then_inc(s_rid, 1)
                pool.wait_ge(s_rid, n + 1)
                pool.wait_ge(s_pos, pair + 1)
                pool.sem_inc(s_turn_pool, 1)
                for b in range(UB):
                    g = UB * (q % 2) + b
                    pool.indirect_dma_start(rows_dram,
                                            bass.IndirectOffsetOnAxis(ap=pos[:, q // 2, g:g + 1], axis=0),
                                            row[:, q, b], None).then_inc(s_scat[q], 16)

            for q in range(A_DEEP):
                scatter(0, q)
            with pool.Fori(1, A_LOOPS) as k:
                for q in range(A_DEEP):
                    scatter(k, q)

            def scatter_out(k, q):
                m = q % BUFS
                pool.wait_ge(s_ob, number(k, q) + 1)
                pool.sem_inc(s_turn_pool, 1)
                for j in range(tiles(k, q)):
                    pool.indirect_dma_start(out, bass.IndirectOffsetOnAxis(ap=out_ids[:, m, j:j + 1], axis=0),
                                            ob[:, m, j], None, bounds_check=TOKENS - 1, oob_is_err=False)\
                        .then_inc(s_out[m], 16)

            for q in range(LATE, C_DEEP):
                scatter_out(0, q)
            with pool.Fori(1, C_LOOPS + 1) as k:
                for q in range(C_DEEP):
                    scatter_out(k, q)

        @block.scalar
        def _(act):
            act.dma_start(w_in[:, 0], W_rel).then_inc(s_small, 16)
            act.dma_start(w_in[:, 1], W_root).then_inc(s_small, 16)
            act.dma_start(gam[:, :], gamma[:, None]).then_inc(s_small, 16)
            act.dma_start(bet[:, :], beta[:, None]).then_inc(s_small, 16)
            act.dma_start(brel_b[:, :], b_rel[None, :].to_broadcast([P, P])).then_inc(s_small, 16)
            act.dma_start(wg_in[:, :], Wg).then_inc(s_small, 16)
            act.dma_start(bgb[:, :], bg[None, :].to_broadcast([P, E])).then_inc(s_small, 16)

            def adj_transposed(k, q):
                n, t = A_DEEP * k + q, q % 2
                act.wait_ge(s_psa, n + 1)
                if unit(k, q, 2):
                    act.wait_ge(s_conv, n - 1)
                act.activation(aT[:, t], ps_a, ACT.Copy).then_inc(s_aT, 1)

            def products_copied(k, q):
                n, t = A_DEEP * k + q, q % 2
                act.wait_ge(s_pspr, n + 1)
                if unit(k, q, 2):
                    act.wait_ge(s_conv, n - 1)
                act.activation(pr[:, t], ps_p, ACT.Copy).then_inc(s_pr, 1)

            def normed(k, q):
                n, t = A_DEEP * k + q, q % 2
                act.wait_ge(s_coef, n + 1)
                if unit(k, q, 2):
                    act.wait_ge(s_psz, n - 1)
                for b in range(UB):
                    last = act.activation(z[:, t, b], xin[:, q % LOADS, b], ACT.Identity,
                                          bias=bias[:, q % 4, 1, b:b + 1], scale=rstd1[:, q % 4, 1, b:b + 1])
                last.then_inc(s_z, 1)

            def z_transposed(k, q):
                n, t = A_DEEP * k + q, q % 2
                act.wait_ge(s_psz, n + 1)
                if unit(k, q, 2):
                    act.wait_ge(s_conv, n - 1)
                act.activation(zT[:, t], ps_z, ACT.Copy).then_inc(s_zT, 1)

            def x1_transposed(k, q):
                n, t = A_DEEP * k + q, q % 2
                act.wait_ge(s_psx1, n + 1)
                if unit(k, q, 2):
                    act.wait_ge(s_gate, n - 1)
                act.activation(x1T[:, t], ps_x1, ACT.Copy).then_inc(s_x1T, 1)

            def residual(k, q):
                n, t = A_DEEP * k + q, q % 2
                if unit(k, q, 2):
                    act.wait_ge(s_x1, n - 1)
                for b in range(UB - 1):
                    last = act.activation(xr[:, t, b], xin[:, q % LOADS, b], ACT.Identity,
                                          bias=bias[:, q % 4, 0, b:b + 1], scale=xr_scale[:, q % 4, b:b + 1])
                last.then_inc(s_xr, 1)

            def stds1(k, q):
                n, t = A_DEEP * k + q, q % 2
                act.wait_ge(s_var1, n + 1)
                act.activation(std1[:, t], var1[:, t], ACT.Sqrt).then_inc(s_std1, 1)

            def stds2(k, q):
                n, t = A_DEEP * k + q, q % 2
                act.wait_ge(s_var2, n + 1)
                act.activation(std2[:, t], var2[:, t], ACT.Sqrt).then_inc(s_std2, 1)

            def slots(k):
                for q in range(A_DEEP):
                    if unit(k, q, 2):
                        products_copied(*back(k, q, 2, A_DEEP))
                    if unit(k, q, 4):
                        stds2(*back(k, q, 4, A_DEEP))
                    if unit(k, q, 1):
                        normed(*back(k, q, 1, A_DEEP))
                        adj_transposed(*back(k, q, 1, A_DEEP))
                    if unit(k, q, 3):
                        x1_transposed(*back(k, q, 3, A_DEEP))
                    if unit(k, q, 1):
                        z_transposed(*back(k, q, 1, A_DEEP))
                    if unit(k, q):
                        stds1(k, q)
                    if unit(k, q, 2):
                        residual(*back(k, q, 2, A_DEEP))

            slots(0)
            with act.Fori(1, A_LOOPS) as k:
                slots(k)
            slots(A_LOOPS)

            def second_weights(k, q):
                n, m = number(k, q), q % BUFS
                if chunk(k, q, BUFS):
                    act.wait_ge(s_y, n + 1 - BUFS)
                e = act.value_load(chunk_tab[0:1, bass.ds(4 * n + 2, 1)], min_val=0, max_val=E - 1)
                skip = LEFT_OUT[tiles(k, q)]
                if skip:
                    act.activation(w1buf[:, m, 1], w1_hl[:, bass.ds(e, 1)].rearrange("p o w c -> p (o w) c"), ACT.Copy)
                act.activation(wbuf[:, m, 1, skip:PACK],
                               experts[:, bass.ds(e, 1), skip:PACK].rearrange("p o c -> p (o c)"), ACT.Copy)\
                    .then_inc(s_w2, 1)

            def chunk_xT(k, q):
                n, t = number(k, q), q % 2
                act.wait_ge(s_psxs, n + 1)
                if chunk(k, q, 2):
                    act.wait_ge(s_h, n - 1)
                act.activation(xsT[:, t, 0], ps_xs[t], ACT.Copy).then_inc(s_xsT, 1)

            def gelus(k, q):
                n, t, m, size = number(k, q), q % 2, q % BUFS, tiles(k, q) * P
                act.wait_ge(s_w, n + 1)
                act.wait_ge(s_h, n + 1)
                if chunk(k, q, 2):
                    act.wait_ge(s_y, n - 1)
                for s in range(2):
                    for h in range(HT):
                        last = act.activation(gT[:, t, s, h, 0:size], ps_h[t][s][:, h, 0:size], ACT.Gelu,
                                              bias=wbuf[:, m, s, PACK - HT + h:PACK - HT + h + 1])
                last.then_inc(s_gel, 1)

            def chunk_slots(k):
                for q in range(C_DEEP):
                    if chunk(k, q):
                        second_weights(k, q)
                    if chunk(k, q) and tiles(k, q) == CJ:
                        chunk_xT(k, q)
                    if chunk(k, q, 1):
                        gelus(*back(k, q, 1, C_DEEP))

            act.activation(gelu_warm[:, :], zero_g[:, 0:1], ACT.Gelu)
            act.wait_ge(s_tbm, 16)
            act.wait_ge(s_exp, 16 * EXPERT_LOADS)
            act.wait_ge(s_b2, 2)
            chunk_slots(0)
            with act.Fori(1, C_LOOPS + 1) as k:
                chunk_slots(k)
            chunk_slots(C_LOOPS + 1)

        @block.vector
        def _(dve):
            dve.wait_ge(s_tab, 16)
            dve.wait_ge(s_ready, 4)
            dve.tensor_copy(tri[:, :], tab[:, T_TRI:T_TRI + P]).then_inc(s_setup, 1)
            dve.tensor_scalar(tri_rest[:, :], tab[:, T_TRI:T_TRI + P], -1.0, 1.0, ALU.mult, ALU.add)\
                .then_inc(s_setup, 1)
            dve.tensor_copy(base_row[:, :, :], tab[0:1, None, T_BASE:T_BASE + NG].to_broadcast([1, PB, NG]))\
                .then_inc(s_setup, 1)
            dve.tensor_scalar(center[:, :], ident, -1.0 / P, None, ALU.add).then_inc(s_setup, 1)

            def fold_weights():
                dve.wait_ge(s_small, 16 * SMALL)
                dve.tensor_scalar(w_gam[:, :, :], w_in[:, :, :], gam[:, :], None, ALU.mult).then_inc(s_setup, 1)
                dve.tensor_copy(bet_mat[:, :], bet[:, :].to_broadcast([P, P])).then_inc(s_setup, 1)

            def fold_constants():
                dve.wait_ge(s_fold, 1)
                dve.tensor_copy(const_b[:, 0], ps_cb[:, 0]).then_inc(s_const, 1)
                dve.tensor_tensor(const_b[:, 1], ps_cb[:, 1], brel_b[:, :], ALU.add).then_inc(s_const, 1)
                dve.tensor_copy(wg[:, :], ps_wg).then_inc(s_const, 1)
                dve.wait_ge(s_const, 3)
                dve.tensor_copy(const_hml[:, 0], const_b[:, :, :]).then_inc(s_const, 1)
                dve.wait_ge(s_const, 4)
                dve.tensor_tensor(part[:, :, :], const_b[:, :, :], const_hml[:, 0], ALU.subtract).then_inc(s_const, 1)
                dve.wait_ge(s_const, 5)
                dve.tensor_copy(const_hml[:, 1], part[:, :, :]).then_inc(s_const, 1)
                dve.wait_ge(s_const, 6)
                dve.tensor_tensor(part[:, :, :], part[:, :, :], const_hml[:, 1], ALU.subtract).then_inc(s_const, 1)
                dve.wait_ge(s_const, 7)
                dve.tensor_copy(const_hml[:, 2], part[:, :, :]).then_inc(s_const, 1)
                dve.wait_ge(s_const, 8)
                dve.tensor_scalar(const_k[:, :, :], const_hml[:, 0], tab[:, T_IDENT:T_IDENT + 1], None, ALU.mult)\
                    .then_inc(s_const, 1)
                for i in range(1, 3):
                    dve.wait_ge(s_const, 8 + i)
                    dve.scalar_tensor_tensor(const_k[:, :, :], const_hml[:, i], tab[:, T_IDENT + i:T_IDENT + i + 1],
                                             const_k[:, :, :], ALU.mult, ALU.add).then_inc(s_const, 1)

            w_bc = tab[:, None, T_W:T_W + E].to_broadcast([P, PB, E])

            def x1(k, q):
                n, t = A_DEEP * k + q, q % 2
                dve.wait_ge(s_conv, n + 1)
                dve.wait_ge(s_xr, n + 1)
                dve.wait_ge(s_xr_last, n + 1)
                if unit(k, q, A_DEEP):
                    dve.wait_ge(s_scat[q], 16 * UB * k)
                dve.scalar_tensor_tensor(row[:, q, :, 0:P], ps_c[t], 0.0, xr[:, t], ALU.max, ALU.add)\
                    .then_inc(s_x1, 1)

            def stats1(k, q, b):
                m = q % LOADS
                if b == 0:
                    dve.wait_ge(s_x[m], 16 * (A_DEEP // LOADS * k + q // LOADS + 1))
                last = dve.bn_stats(st1[:, q % 2, b], xin[:, m, b])
                if b == UB - 1:
                    last.then_inc(s_bn1, 1)

            def aggregate1(k, q):
                dve.wait_ge(s_bn1, 2 * (A_DEEP * k + q) + 1)
                dve.sem_inc(s_turn_dve, 1)
                for b in range(UB):
                    last = dve.bn_aggr(mv1[:, q % 2, b], st1[:, q % 2, b])
                last.then_inc(s_bn1, 1)

            def variances1(k, q):
                n, t = A_DEEP * k + q, q % 2
                dve.wait_ge(s_bn1, 2 * n + 2)
                dve.tensor_scalar(var1[:, t, 0], mv1[:, t, :, 1], EPS, None, ALU.add)
                dve.tensor_scalar(var1[:, t, 1], mv1[:, t, :, 1], 1.0 + EPS, EPS * EPS, ALU.mult, ALU.add)\
                    .then_inc(s_var1, 1)

            def rstds1(k, q):
                dve.wait_ge(s_std1, A_DEEP * k + q + 1)
                dve.reciprocal(rstd1[:, q % 4], std1[:, q % 2]).then_inc(s_rstd1, 1)

            def coefs(k, q):
                n, m = A_DEEP * k + q, q % 4
                dve.wait_ge(s_rstd1, n + 1)
                dve.tensor_scalar(xr_scale[:, m], rstd1[:, m, 0], 1.0, None, ALU.add)
                dve.scalar_tensor_tensor(bias[:, m], mv1[:, q % 2, None, :, 0].to_broadcast([P, 2, UB]), -1.0,
                                         rstd1[:, m], ALU.mult, ALU.mult).then_inc(s_coef, 1)

            def last_residual(k, q):
                m, b = q % 4, UB - 1
                dve.wait_ge(s_coef, A_DEEP * k + q + 1)
                dve.tensor_scalar(xr[:, q % 2, b], xin[:, q % LOADS, b], xr_scale[:, m, b:b + 1],
                                  bias[:, m, 0, b:b + 1], ALU.mult, ALU.add).then_inc(s_xr_last, 1)

            def stats2(k, q, b):
                if b == 0:
                    dve.wait_ge(s_x1, A_DEEP * k + q + 1)
                last = dve.bn_stats(st2[:, q % 2, b], row[:, q, b, 0:P])
                if b == UB - 1:
                    last.then_inc(s_bn2, 1)

            def aggregate2_wait(k, q):
                dve.wait_ge(s_bn2, 2 * (A_DEEP * k + q) + 1)
                dve.sem_inc(s_turn_dve, 1)

            def aggregate2(k, q, b):
                last = dve.bn_aggr(row[:, q, b, MEAN:VAR + 1], st2[:, q % 2, b])
                if b == UB - 1:
                    last.then_inc(s_bn2, 1)

            def variances2(k, q):
                dve.wait_ge(s_bn2, 2 * (A_DEEP * k + q) + 2)
                dve.tensor_scalar(var2[:, q % 2], row[:, q, :, VAR], EPS, None, ALU.add).then_inc(s_var2, 1)

            def rstds2(k, q):
                dve.wait_ge(s_std2, A_DEEP * k + q + 1)
                dve.reciprocal(row[:, q, :, RSTD], std2[:, q % 2]).then_inc(s_rstd2, 1)

            TOP_STEPS = 12

            def top2(pair, q):

                def per_graph(v):
                    return v[:, :, None].to_broadcast([P, PB, E])

                base = TOP_STEPS * pair

                def after(i):
                    dve.wait_ge(s_top, base + i)

                dve.wait_ge(s_gate, 2 * pair + 2)
                dve.wait_ge(s_rstd2, 2 * pair + 2)
                dve.tensor_tensor(gx[:, :, :].rearrange("p (t b) e -> p t b e", t=2),
                                  ps_g.rearrange("p (t b) e -> p t b e", t=2),
                                  row[:, q:q + 2, :, RSTD:RSTD + 1].to_broadcast([P, 2, UB, E]), ALU.mult)\
                    .then_inc(s_gread, 1)
                yield
                dve.wait_ge(s_gread, pair + 1)
                dve.tensor_tensor(g1[:, :, :], gx[:, :, :], bgb[:, None, :].to_broadcast([P, PB, E]), ALU.add)\
                    .then_inc(s_top, 1)
                yield
                after(1)
                dve.tensor_reduce(m1[:, :], g1[:, :, :], AX.X, ALU.max).then_inc(s_top, 1)
                yield
                after(2)
                dve.tensor_tensor(eq[:, :, :], g1[:, :, :], per_graph(m1), ALU.is_equal).then_inc(s_top, 1)
                yield
                after(3)
                dve.tensor_tensor(eqw[:, :, :], eq[:, :, :], w_bc, ALU.mult).then_inc(s_top, 1)
                yield
                after(4)
                dve.tensor_reduce(w1[:, :], eqw[:, :, :], AX.X, ALU.max).then_inc(s_top, 1)
                yield
                after(5)
                dve.tensor_tensor(eq[:, :, :], w_bc, per_graph(w1), ALU.is_equal).then_inc(s_top, 1)
                yield
                after(6)
                dve.scalar_tensor_tensor(g2[:, :, :], eq[:, :, :], -BIG, g1[:, :, :], ALU.mult, ALU.add)\
                    .then_inc(s_top, 1)
                yield
                after(7)
                dve.tensor_reduce(m2[:, :], g2[:, :, :], AX.X, ALU.max).then_inc(s_top, 1)
                yield
                after(8)
                dve.tensor_tensor(eq[:, :, :], g2[:, :, :], per_graph(m2), ALU.is_equal).then_inc(s_top, 1)
                yield
                after(9)
                dve.tensor_tensor(eqw[:, :, :], eq[:, :, :], w_bc, ALU.mult).then_inc(s_top, 1)
                yield
                after(10)
                dve.tensor_reduce(w2[:, :], eqw[:, :, :], AX.X, ALU.max).then_inc(s_top, 1)
                yield
                after(11)
                dve.tensor_tensor(code[:, :], w1[:, :], w2[:, :], ALU.add).then_inc(s_top, 1)
                yield

            def mark(pair):
                dve.wait_ge(s_top, TOP_STEPS * pair + TOP_STEPS)
                if not isinstance(pair, int) or pair > 0:
                    dve.wait_ge(s_cnt, pair)
                dve.tensor_tensor(onehot[:, :, :], tab[:, None, T_CODE:T_CODE + NG].to_broadcast([P, PB, NG]),
                                  code[:, :, None].to_broadcast([P, PB, NG]), ALU.is_equal).then_inc(s_hot, 1)

            def ranks_of_own(pair):
                dve.wait_ge(s_rank, pair + 1)
                dve.tensor_tensor(rank_m[:, :, :], ps_r, onehot[:, :, :], ALU.mult).then_inc(s_rread, 1)

            def positions(pair, buf):
                dve.wait_ge(s_rread, pair + 1)
                with nc.allow_low_precision(reason="whole numbers below 2^24, summed in float32"):
                    dve.tensor_reduce(pos[:, buf], rank_m[:, :, :], AX.X, ALU.add).then_inc(s_pos, 1)

            def slots(k):
                for q in range(A_DEEP):
                    choosing = q % 2 == 1 and unit(k, q, 5)
                    placing = q % 2 == 0 and unit(k, q, 6)
                    pair = A_DEEP // 2 * k + q // 2 - (2 if q % 2 else 3)
                    choice = top2(pair, (q - 5) % A_DEEP) if choosing else iter(())
                    if unit(k, q):
                        for b in range(UB):
                            stats1(k, q, b)
                    if placing:
                        mark(pair)
                    if unit(k, q, 2):
                        last_residual(*back(k, q, 2, A_DEEP))
                    if unit(k, q, 3):
                        x1(*back(k, q, 3, A_DEEP))
                    if unit(k, q, 4):
                        rstds2(*back(k, q, 4, A_DEEP))
                    next(choice, None)
                    if unit(k, q):
                        aggregate1(k, q)
                    next(choice, None)
                    if unit(k, q):
                        variances1(k, q)
                    for b in range(UB):
                        next(choice, None)
                        if unit(k, q, 3):
                            stats2(*back(k, q, 3, A_DEEP), b)
                    next(choice, None)
                    if placing:
                        ranks_of_own(pair)
                    if unit(k, q, 3):
                        aggregate2_wait(*back(k, q, 3, A_DEEP))
                    for b in range(UB):
                        if unit(k, q, 3):
                            aggregate2(*back(k, q, 3, A_DEEP), b)
                        next(choice, None)
                    if placing:
                        positions(pair, (q // 2 + 1) % 4)
                    if unit(k, q, 3):
                        variances2(*back(k, q, 3, A_DEEP))
                    next(choice, None)
                    if isinstance(k, int) and A_DEEP * k + q == 1:
                        fold_constants()
                    if unit(k, q):
                        rstds1(k, q)
                    next(choice, None)
                    if unit(k, q):
                        coefs(k, q)
                    for _ in choice:
                        pass
                    if isinstance(k, int) and k + q == 0:
                        fold_weights()
            slots(0)
            with dve.Fori(1, A_LOOPS) as k:
                slots(k)
            slots(A_LOOPS)

            STEPS = 0

            def step(ins):
                nonlocal STEPS
                STEPS += 1
                ins.then_inc(s_tb, 1)
                dve.wait_ge(s_tb, STEPS)

            base = tab[:, T_BASE:T_BASE + NG]
            wide_no = tab[:, T_PAIR:T_PAIR + 1]
            narrow_no = tab[:, T_SINGLE:T_SINGLE + 1]
            vals = tab[:, T_VALS:T_VALS + 5 * NG].rearrange("p (v g) -> p v g", v=5)
            dve.wait_ge(s_cnt, UNITS // 2)
            step(dve.tensor_tensor(cnt[:, :], ps_r[:, 0], base, ALU.subtract))
            step(dve.tensor_scalar(cnt_up[:, :], cnt[:, :], float(P - 1), None, ALU.add))
            dve.tensor_scalar(halves_i[:, 0], cnt_up[:, :], C.bit_length() - 1, None, ALU.logical_shift_right)
            step(dve.tensor_scalar(halves_i[:, 1], cnt_up[:, :], P.bit_length() - 1, 1, ALU.logical_shift_right,
                                   ALU.bitwise_and))
            step(dve.tensor_copy(halves[:, :, :], halves_i[:, :, :]))
            for w in (1, 0):
                last = dve.tensor_tensor_scan(c_end[:, w], halves[:, w], zero_g[:, :], 0.0, ALU.add, ALU.add)
            step(last)
            dve.tensor_tensor(c_beg[:, :, :], c_end[:, :, :], halves[:, :, :], ALU.subtract)
            step(dve.tensor_scalar(over[:, :], narrow_no, c_end[:, 1, NG - 1:NG], None, ALU.subtract))
            dve.tensor_scalar(is_over[:, :], over[:, :], 0.0, None, ALU.is_ge)
            step(dve.tensor_scalar(over_i[:, :], over[:, :], 0.0, None, ALU.max))
            dve.tensor_scalar(over_parts_i[:, 0:1], over_i[:, :], 1, None, ALU.logical_shift_right)
            step(dve.tensor_scalar(over_parts_i[:, 1:2], over_i[:, :], 1, None, ALU.bitwise_and))
            step(dve.tensor_copy(over_parts[:, :], over_parts_i[:, :]))
            step(dve.scalar_tensor_tensor(pair_no[:, :], over_parts[:, 0:1], float(WIDE + 1), is_over[:, :],
                                          ALU.add, ALU.mult))
            step(dve.tensor_tensor(pair_no[:, :], pair_no[:, :], wide_no, ALU.add))
            step(dve.scalar_tensor_tensor(pair_at[:, :], over_parts[:, 1:2], P / C, pair_no[:, :],
                                          ALU.mult, ALU.add))
            for w, no in ((0, pair_no[:, :]), (1, narrow_no)):
                dve.tensor_scalar(in_beg[:, w], c_beg[:, w], no, None, ALU.is_le)
                dve.tensor_scalar(in_end[:, w], c_end[:, w], no, None, ALU.is_gt)
            dve.tensor_scalar(at_both[:, 0], c_beg[:, 0], pair_at[:, :], -float(C), ALU.subtract, ALU.mult)
            dve.tensor_scalar(at_both[:, 1], halves[:, 0], float(C), None, ALU.mult)
            step(dve.tensor_scalar(last_at[:, :], cnt[:, :], tab[:, T_SIZE:T_SIZE + 1], None, ALU.subtract))
            step(dve.tensor_tensor(in_both[:, :, :], in_beg[:, :, :], in_end[:, :, :], ALU.mult))
            dve.tensor_tensor(in_g[:, :], in_both[:, 0], in_both[:, 1], ALU.add)
            step(dve.tensor_tensor(at_both[:, :, :], at_both[:, :, :], in_both[:, :, :], ALU.mult))
            step(dve.tensor_tensor(at[:, :], at_both[:, 0], at_both[:, 1], ALU.add))
            step(dve.tensor_tensor(near[:, :], at[:, :], last_at[:, :], ALU.min))
            dve.tensor_tensor(vals[:, 4], at[:, :], near[:, :], ALU.subtract)
            step(dve.tensor_tensor(vals[:, 0], near[:, :], base, ALU.add))
            step(dve.tensor_tensor(picked[:, :, :], vals, in_g[:, None, :].to_broadcast([P, 5, NG]), ALU.mult))
            with nc.allow_low_precision(reason="whole numbers below 2^24, summed in float32"):
                dve.tensor_reduce(chunk_cols[:, :], picked[:, :, :], AX.X, ALU.add).then_inc(s_tbd, 1)
            dve.wait_ge(s_tbd, 1)
            dve.tensor_scalar(repeated[:, :], ident, chunk_cols[:, 4:5], None, ALU.mult).then_inc(s_rep, 1)
            dve.wait_ge(s_repb, 1)
            dve.tensor_tensor(drop[:, :, :], tab[:, None, T_ROW:T_ROW + CJ].to_broadcast([P, P, CJ]),
                              bank[0][:, 0:P, None].to_broadcast([P, P, CJ]), ALU.is_lt).then_inc(s_rep, 1)
            dve.wait_ge(s_rep, 2)
            dve.tensor_tensor(drop[:, NARROW_CHUNKS, 0],
                              tab[:, T_ROW + CJ:T_ROW + CJ + 1].to_broadcast([P, NARROW]),
                              bank[0][:, NARROW_CHUNKS], ALU.is_lt).then_inc(s_rep, 1)
            dve.wait_ge(s_rep, 3)
            dve.tensor_scalar(drop[:, :, :], drop[:, :, :], float(TOKENS), None, ALU.mult).then_inc(s_rep, 1)
            dve.wait_ge(s_rep, 4)
            dve.wait_ge(s_tbm, 16)
            dve.wait_ge(s_b2, 2)

            def value(n, v, top):
                return dve.value_load(chunk_tab[0:1, bass.ds(4 * n + v, 1)], min_val=0, max_val=top)

            def prepare(k, q, e, g):
                n, t, m, nt = number(k, q), q % 2, q % BUFS, tiles(k, q)
                if chunk(k, q, BUFS):
                    dve.wait_ge(s_y, n + 1 - BUFS)
                skip = LEFT_OUT[nt]
                if skip:
                    dve.tensor_copy(w1buf[:, m, 0], w1_hl[:, bass.ds(e, 1)].rearrange("p o w c -> p (o w) c"))
                dve.tensor_copy(wbuf[:, m, 0, skip:PACK],
                                experts[:, bass.ds(e, 1), skip:PACK].rearrange("p o c -> p (o c)")).then_inc(s_w, 1)
                dve.wait_ge(s_rows[m], 16 * (C_DEEP // BUFS * k + q // BUFS + 1 - LATE // BUFS))
                if chunk(k, q, 2):
                    dve.wait_ge(s_psxs, n - 1)
                for j in range(nt):
                    last = dve.tensor_scalar(xs[:, t, j], rows[:, m, j, 0:P], rows[:, m, j, MEAN:MEAN + 1],
                                             rows[:, m, j, RSTD:RSTD + 1], ALU.subtract, ALU.mult)
                last.then_inc(s_xs, 1)
                if chunk(k, q, BUFS):
                    dve.wait_ge(s_ob, n + 1 - BUFS)
                dve.tensor_tensor(row_ids[:, m, 0:nt], rows_u[:, m, 0:nt, ID],
                                  drop[:, bass.ds(n, 1), 0:nt].rearrange("p o j -> p (o j)"), ALU.add)\
                    .then_inc(s_ids, 1)
                dve.tensor_tensor(xb[:, m, 0:nt], rows[:, m, 0:nt, 0:P],
                                  b2_pair[:, bass.ds(g, 1)].to_broadcast([P, nt, P]), ALU.add).then_inc(s_xb, 1)

            def low_part(k, q):
                n, t = number(k, q), q % 2
                if tiles(k, q) < CJ:
                    dve.wait_ge(s_psxs, n + 1)
                    if chunk(k, q, 3):
                        dve.wait_ge(s_h, n - 2)
                    dve.tensor_copy(xsT_narrow[:, :], ps_xs[t][:, 0:P]).then_inc(s_xsL, 1)
                    return
                dve.wait_ge(s_xsT, wide_chunks(k, q))
                dve.tensor_tensor(xsT[:, t, 1], ps_xs[t], xsT[:, t, 0].bitcast(F32), ALU.subtract)\
                    .then_inc(s_xsL, 1)

            def finish(k, q):
                n, t, m, nt = number(k, q), q % 2, q % BUFS, tiles(k, q)
                dve.wait_ge(s_y, n + 1)
                if chunk(k, q, BUFS):
                    dve.wait_ge(s_out[m], scattered(k, q))
                dve.wait_ge(s_ids, n + 1)
                dve.tensor_copy(out_ids[:, m, 0:nt], row_ids[:, m, 0:nt])
                dve.wait_ge(s_xb, n + 1)
                dve.tensor_tensor(ob[:, m, 0:nt], ps_y[t][:, 0:nt], xb[:, m, 0:nt], ALU.add).then_inc(s_ob, 1)

            def chunk_slots(k):
                for q in range(C_DEEP):
                    if chunk(k, q):
                        e, g = value(number(k, q), 1, E - 1), value(number(k, q), 3, NG - 1)
                    if chunk(k, q, 4):
                        finish(*back(k, q, 4, C_DEEP))
                    if chunk(k, q):
                        prepare(k, q, e, g)
                    if chunk(k, q, 1):
                        low_part(*back(k, q, 1, C_DEEP))

            chunk_slots(0)
            with dve.Fori(1, C_LOOPS + 1) as k:
                chunk_slots(k)
            chunk_slots(C_LOOPS + 1)

        @block.tensor
        def _(pe):
            def adj_transposes(k, q):
                n, m = A_DEEP * k + q, q % LOADS
                pe.wait_ge(s_adj[m], 16 * (A_DEEP // LOADS * k + q // LOADS + 1))
                if unit(k, q, 1):
                    pe.wait_ge(s_aT, n)
                for b in range(UB):
                    last = pe.transpose(ps_a[:, b], ain[:, m, b], ident)
                last.then_inc(s_psa, 1)

            def z_transposes(k, q):
                n, t = A_DEEP * k + q, q % 2
                pe.wait_ge(s_z, n + 1)
                if unit(k, q, 1):
                    pe.wait_ge(s_zT, n)
                for b in range(UB):
                    last = pe.transpose(ps_z[:, b], z[:, t, b], ident)
                last.then_inc(s_psz, 1)

            def products(k, q):
                n, t = A_DEEP * k + q, q % 2
                pe.wait_ge(s_zT, n + 1)
                if unit(k, q, 1):
                    pe.wait_ge(s_pr, n)
                else:
                    pe.wait_ge(s_const, 11)
                pe.matmul(ps_p, ones[:, :], const_k[:, 0, None, :].to_broadcast([P, UB, P]), start=True, stop=False,
                          skip_group_check=True)
                for b in range(UB):
                    last = pe.matmul(ps_p[:, b], zT[:, t, b], w_gam[:, 0], start=False, stop=b == UB - 1,
                                     skip_group_check=True)
                last.then_inc(s_pspr, 1)

            def conv(k, q):
                n, t = A_DEEP * k + q, q % 2
                if unit(k, q, 2):
                    pe.wait_ge(s_x1, n - 1)
                pe.matmul(ps_c[t], ones[:, :], const_k[:, 1, None, :].to_broadcast([P, UB, P]), start=True, stop=False,
                          skip_group_check=True)
                pe.wait_ge(s_zT, n + 1)
                for b in range(UB):
                    pe.matmul(ps_c[t][:, b], zT[:, t, b], w_gam[:, 1], start=False, stop=False,
                              skip_group_check=True)
                pe.wait_ge(s_aT, n + 1)
                pe.wait_ge(s_pr, n + 1)
                for b in range(UB):
                    last = pe.matmul(ps_c[t][:, b], aT[:, t, b], pr[:, t, b], start=False, stop=b == UB - 1,
                                     skip_group_check=True)
                last.then_inc(s_conv, 1)

            def x1_transposes(k, q):
                n = A_DEEP * k + q
                pe.wait_ge(s_x1, n + 1)
                if unit(k, q, 1):
                    pe.wait_ge(s_x1T, n)
                for b in range(UB):
                    last = pe.transpose(ps_x1[:, b], row[:, q, b, 0:P], ident)
                last.then_inc(s_psx1, 1)

            def gates(k, q):
                n, t = A_DEEP * k + q, q % 2
                pe.wait_ge(s_x1T, n + 1)
                if t == 0 and unit(k, q, 1):
                    pe.wait_ge(s_gread, A_DEEP // 2 * k + q // 2)
                for b in range(UB):
                    last = pe.matmul(ps_g[:, UB * t + b], x1T[:, t, b], wg[:, :], start=True, stop=True)
                last.then_inc(s_gate, 1)

            def ranks(pair):
                pe.wait_ge(s_hot, pair + 1)
                last = pe.matmul(ps_r, tri[:, :], onehot[:, :, :], start=False, stop=False, skip_group_check=True)
                for b in range(PB - 1):
                    m = PB - 1 - b
                    last = pe.matmul(ps_r[:, b + 1:PB], ones[:, :], onehot[:, b:b + 1].to_broadcast([P, m, NG]),
                                     start=False, stop=False, skip_group_check=True)
                last.then_inc(s_rank, 1)

            def counts(pair):
                pe.wait_ge(s_rread, pair + 1)
                pe.matmul(ps_r, tri_rest[:, :], onehot[:, :, :], start=False, stop=False, skip_group_check=True)
                for b in range(1, PB):
                    last = pe.matmul(ps_r[:, 0:b], ones[:, :], onehot[:, b:b + 1].to_broadcast([P, b, NG]),
                                     start=False, stop=False, skip_group_check=True)
                last.then_inc(s_cnt, 1)

            def slots(k):
                for q in range(A_DEEP):
                    pair = A_DEEP // 2 * k + q // 2 - 3
                    if unit(k, q, 2):
                        conv(*back(k, q, 2, A_DEEP))
                    if unit(k, q, 3):
                        x1_transposes(*back(k, q, 3, A_DEEP))
                    if q % 2 == 0 and unit(k, q, 6):
                        ranks(pair)
                    if unit(k, q, 1):
                        z_transposes(*back(k, q, 1, A_DEEP))
                    if q % 2 == 1 and unit(k, q, 7):
                        counts(pair)
                    if unit(k, q, 3):
                        gates(*back(k, q, 3, A_DEEP))
                    if unit(k, q, 1):
                        products(*back(k, q, 1, A_DEEP))
                    if unit(k, q):
                        adj_transposes(k, q)

            pe.wait_ge(s_tab, 16)
            pe.wait_ge(s_ready, 4)
            pe.wait_ge(s_setup, 6)
            pe.matmul(ps_r, ones_row[:, :], base_row[:, :, :], start=True, stop=False, skip_group_check=True)
            pe.matmul(ps_cb, bet_mat[:, :], w_in[:, :, :], start=True, stop=True)
            pe.matmul(ps_wg, center[:, :], wg_in[:, :], start=True, stop=True).then_inc(s_fold, 1)
            slots(0)
            with pe.Fori(1, A_LOOPS) as k:
                slots(k)
            slots(A_LOOPS)

            pe.wait_ge(s_rep, 1)
            pe.matmul(bank[0][:, 0:P], ones_f[:, :], repeated[:, :], start=True, stop=True).then_inc(s_repb, 1)

            def chunk_transpose(k, q):
                n, t, nt = number(k, q), q % 2, tiles(k, q)
                pe.wait_ge(s_xs, n + 1)
                if chunk(k, q, 2):
                    pe.wait_ge(s_xsL, n - 1)
                for j in range(nt):
                    last = pe.transpose(ps_xs[t][:, j * P:(j + 1) * P], xs[:, t, j], ident)
                last.then_inc(s_psxs, 1)

            def up(k, q):
                n, t, m = number(k, q), q % 2, q % BUFS
                pe.wait_ge(s_w, n + 1)
                pe.wait_ge(s_w2, n + 1)
                pe.wait_ge(s_xsL, n + 1)
                if chunk(k, q, 2):
                    pe.wait_ge(s_gel, n - 1)
                for s in range(2):
                    for h in range(HT):
                        if tiles(k, q) < CJ:
                            last = pe.matmul(ps_h[t][s][:, h, 0:P], wbuf[:, m, s, h * P:(h + 1) * P],
                                             xsT_narrow[:, :], start=True, stop=True)
                            continue
                        for w, v in ((0, 0), (0, 1), (1, 0)):
                            last = pe.matmul(ps_h[t][s][:, h], w1buf[:, m, s, w, h * P:(h + 1) * P],
                                             xsT[:, t, v], start=w + v == 0, stop=w == 1)
                last.then_inc(s_h, 1)

            def down(k, q):
                n, t, m, nt = number(k, q), q % 2, q % BUFS, tiles(k, q)
                pe.wait_ge(s_gel, n + 1)
                if chunk(k, q, 2):
                    pe.wait_ge(s_ob, n - 1)
                for j in range(nt):
                    for s in range(2):
                        for h in range(HT):
                            last = pe.matmul(ps_y[t][:, j], gT[:, t, s, h, j * P:(j + 1) * P],
                                             wbuf[:, m, s, HID + h * P:HID + (h + 1) * P],
                                             start=s + h == 0, stop=s + h == HT)
                last.then_inc(s_y, 1)

            def chunk_slots(k):
                for q in range(C_DEEP):
                    if chunk(k, q):
                        chunk_transpose(k, q)
                    if chunk(k, q, 1):
                        up(*back(k, q, 1, C_DEEP))
                    if chunk(k, q, 2):
                        down(*back(k, q, 2, C_DEEP))

            chunk_slots(0)
            with pe.Fori(1, C_LOOPS + 1) as k:
                chunk_slots(k)
            chunk_slots(C_LOOPS + 1)


INPUTS = ["x", "adj", "L0_gnn_W_rel", "L0_gnn_b_rel", "L0_gnn_W_root", "L0_gnn_ln_gamma", "L0_gnn_ln_beta",
          "L0_ffn_Wg", "L0_ffn_bg", "L0_ffn_W1", "L0_ffn_b1", "L0_ffn_W2", "L0_ffn_b2"]


def kernel(**inputs):
    import numpy as _np
    import concourse.bacc as _bacc
    from concourse import mybir as _mybir
    from concourse.bass_utils import run_bass_kernel_spmd as _run

    nc = _bacc.Bacc("TRN2", target_bir_lowering=False, num_devices=1)
    arrays, args = {}, []
    named = [(n, _np.ascontiguousarray(inputs[n])) for n in INPUTS]
    named += list(zip(["shape_table", "token_ids", "padding_rows"], constants()))
    for name, a in named:
        arrays[f"in_{name}"] = a
        args.append(nc.dram_tensor(f"in_{name}", a.shape, _mybir.dt.from_np(a.dtype), kind="ExternalInput").ap())
    out = nc.dram_tensor("out_rows", (TOKENS, P), _mybir.dt.float32, kind="ExternalOutput").ap()
    build(nc, *args, out)
    r = _run(nc, [arrays], core_ids=[0])
    return r.results[0]["out_rows"].reshape(GRAPHS, P, P)
```
